# Optimizing a Trainium2 kernel written in Bass

```python
import numpy as np
import jax
import jax.numpy as jnp

def _softmax(x, axis=-1):
    return jax.nn.softmax(x, axis=axis)

def _gelu(x):
    return jax.nn.gelu(x, approximate=True)

def _silu(x):
    return jax.nn.silu(x)

def _sigmoid(x):
    return jax.nn.sigmoid(x)

def _layernorm(x, axis=-1, eps=1e-05):
    m = jnp.mean(x, axis=axis, keepdims=True)
    v = jnp.var(x, axis=axis, keepdims=True)
    return (x - m) / jnp.sqrt(v + eps)

def _scatter_add(tgt, idx, src, axis=0):
    return tgt.at[idx].add(src)

def _segment_sum(src, seg, n):
    return jax.ops.segment_sum(src, seg, n)
kernel_name = 'mk_adj_preln_d1_adj_r2_899ddf'

def setup_inputs(seed: int=0):
    np.random.seed(seed)
    _w = jnp.asarray

    def _rec_inputs():
        import jax
        import jax.numpy as jnp
        _gk = jax.random.key(seed)
        x = 7.22e-05 + 1 * jax.random.normal(jax.random.fold_in(_gk, 1), (4096, 512), jnp.float32)
        _a = jax.random.bernoulli(jax.random.fold_in(_gk, 2), 0.000976562, (4096, 4096))
        _af = _a.astype(jnp.float32)
        adj = _af
        return (x, adj)
    x, adj = _rec_inputs()

    def _L0_gnn_setup():
        import jax, jax.numpy as jnp
        import numpy as np
        N = 4096
        D = 512
        key = jax.random.key(seed)
        ks = jax.random.split(key, 13)
        w_scale = 1.0 / np.sqrt(D)
        inp = {'query': jax.random.normal(ks[0], (N, D), dtype=jnp.float32), 'key': jax.random.normal(ks[1], (N, D), dtype=jnp.float32), 'value': jax.random.normal(ks[2], (N, D), dtype=jnp.float32), 'adj_matrix': jax.random.randint(ks[3], (N, N), 0, 2).astype(jnp.float32), 'Wq': jax.random.normal(ks[4], (D, D), dtype=jnp.float32) * w_scale, 'bq': jax.random.normal(ks[5], (D,), dtype=jnp.float32) * 0.01, 'Wk': jax.random.normal(ks[6], (D, D), dtype=jnp.float32) * w_scale, 'bk': jax.random.normal(ks[7], (D,), dtype=jnp.float32) * 0.01, 'Wv': jax.random.normal(ks[8], (D, D), dtype=jnp.float32) * w_scale, 'bv': jax.random.normal(ks[9], (D,), dtype=jnp.float32) * 0.01, 'Wm': jax.random.normal(ks[10], (D, D), dtype=jnp.float32) * w_scale, 'bm': jax.random.normal(ks[11], (D,), dtype=jnp.float32) * 0.01}
        return inp
    _L0_gnn_all = _L0_gnn_setup()
    _L0_gnn_in = {k: v for k, v in _L0_gnn_all.items() if k in ('key', 'value', 'Wq', 'bq', 'Wk', 'bk', 'Wv', 'bv', 'Wm', 'bm')}
    del _L0_gnn_all
    return {'x': x, 'adj': adj, 'L0_gnn_key': _L0_gnn_in['key'], 'L0_gnn_value': _L0_gnn_in['value'], 'L0_gnn_Wq': _L0_gnn_in['Wq'], 'L0_gnn_bq': _L0_gnn_in['bq'], 'L0_gnn_Wk': _L0_gnn_in['Wk'], 'L0_gnn_bk': _L0_gnn_in['bk'], 'L0_gnn_Wv': _L0_gnn_in['Wv'], 'L0_gnn_bv': _L0_gnn_in['bv'], 'L0_gnn_Wm': _L0_gnn_in['Wm'], 'L0_gnn_bm': _L0_gnn_in['bm']}

def reference(x, adj, L0_gnn_key, L0_gnn_value, L0_gnn_Wq, L0_gnn_bq, L0_gnn_Wk, L0_gnn_bk, L0_gnn_Wv, L0_gnn_bv, L0_gnn_Wm, L0_gnn_bm):
    import jax
    import jax.numpy as jnp

    def _L0_gnn_ref(query, key, value, adj_matrix, Wq, bq, Wk, bk, Wv, bv, Wm, bm):
        import jax, jax.numpy as jnp
        import numpy as np
        N = 4096
        D = 512
        q = query @ Wq.T + bq
        k = key @ Wk.T + bk
        v = value @ Wv.T + bv
        scale = q.shape[0] ** 0.5
        scores = jnp.einsum('nd,md->nm', q, k) / scale
        adj_scores = scores * adj_matrix
        adj_scores = jnp.where(jnp.abs(adj_scores) < 1e-05, -1000000000.0, adj_scores)
        prob = jax.nn.softmax(adj_scores, axis=-1)
        x = jnp.einsum('nm,md->nd', prob, v)
        return x @ Wm.T + bm
    h = jnp.maximum(_layernorm(x, axis=-1), 0.0)
    x = x + _L0_gnn_ref(h, L0_gnn_key, L0_gnn_value, adj, L0_gnn_Wq, L0_gnn_bq, L0_gnn_Wk, L0_gnn_bk, L0_gnn_Wv, L0_gnn_bv, L0_gnn_Wm, L0_gnn_bm)
    return x

_drawn_inputs = setup_inputs


def setup_inputs(seed=0):
    import zlib

    import numpy as np

    out = dict(_drawn_inputs(seed))
    spreads = {}
    factors = {'L0_gnn_bq': 45.838, 'L0_gnn_bk': 64.0, 'L0_gnn_bv': 6.794, 'L0_gnn_bm': 6.348}
    for name, (base, spread) in spreads.items():
        noise = np.random.default_rng([zlib.crc32(name.encode()), seed]).standard_normal(out[name].shape)
        drawn = base * np.exp(spread * noise) if base else spread * noise
        out[name] = jnp.asarray(drawn.astype(out[name].dtype))
    for name, factor in factors.items():
        out[name] = (out[name] * factor).astype(out[name].dtype)
    return out
```

```python
from contextlib import ExitStack

import concourse.bass as bass
from concourse import mybir

F32 = mybir.dt.float32
ALU = mybir.AluOpType
ACT = mybir.ActivationFunctionType
AX = mybir.AxisListType
P = 128
MASKED = -1e9
THRESHOLD = 1e-5
EPS = 1e-5


def graph_attention(nc, x, adj, keyT, value, wq, wk, wv, wmT, bq, bk, bv, bm, out):
    N, D = x.shape
    T = N // P
    C = D // P
    W = 512
    J = N // W
    G = W // P
    INV = 1.0 / float(N) ** 0.5

    with ExitStack() as ctx:
        def sb(name, shape, dt=F32):
            return ctx.enter_context(nc.sbuf_tensor(name, shape, dt))

        def pb(name, shape, dt=F32):
            return ctx.enter_context(nc.psum_tensor(name, shape, dt))

        def sem(name):
            return ctx.enter_context(nc.semaphore(name))

        keys_T = sb("keys_T", [P, C, N])
        values = sb("values", [P, T, D])
        w_scores = sb("w_scores", [P, C, D])
        w_out = sb("w_out", [P, C, D])
        w_shift = sb("w_shift", [P, C])
        b_scores = sb("b_scores", [P, D])
        b_out = sb("b_out", [P, D])
        b_shift = sb("b_shift", [P, 1])
        ident = sb("ident", [P, P])
        ones = sb("ones", [P, P])
        bias_cols = sb("bias_cols", [P, 3, C])
        bias_wide = sb("bias_wide", [P, 2, C, P])
        half = sb("half", [P, 1])
        x_t = sb("x_t", [P, D])
        adj_t = sb("adj_t", [P, N])
        scores = sb("scores", [P, N])
        below = sb("below", [P, W])
        stats = sb("stats", [P, 6])
        mean_var = sb("mean_var", [P, 2])
        var_eps = sb("var_eps", [P, 1])
        rstd = sb("rstd", [P, 1])
        neg_mean = sb("neg_mean", [P, 1])
        h_t = sb("h_t", [P, D])
        hT = sb("hT", [P, C, P])
        q_t = sb("q_t", [P, D])
        qT = sb("qT", [P, C, P])
        shift = sb("shift", [P, 1])
        shift_scaled = sb("shift_scaled", [P, 1])
        row_max = sb("row_max", [P, 1])
        neg_max = sb("neg_max", [P, 1])
        row_sum = sb("row_sum", [P, 1])
        inv_sum = sb("inv_sum", [P, 1])
        probs_T = sb("probs_T", [P, 2, W])
        ctx_t = q_t
        ctxT = sb("ctxT", [P, C, P])
        x_bias = h_t
        out_t = sb("out_t", [P, D])

        p_turn = pb("p_turn", [P, W])
        p_proj = pb("p_proj", [P, W])
        p_shift = pb("p_shift", [P, W])
        p_scores = [pb(f"p_scores{i}", [P, W]) for i in range(2)]
        p_ctx = pb("p_ctx", [P, W])
        p_probs = [pb(f"p_probs{i}", [P, W]) for i in range(2)]

        weights_in = sem("weights_in")
        keys_in = sem("keys_in")
        values_in = sem("values_in")
        consts_made = sem("consts_made")
        zeros_made = sem("zeros_made")
        wide_made = sem("wide_made")
        products = sem("products")
        products_read = sem("products_read")
        x_in = sem("x_in")
        adj_in = sem("adj_in")
        x_used = sem("x_used")
        adj_used = sem("adj_used")
        stats_step = sem("stats_step")
        stats_made = sem("stats_made")
        rstd_made = sem("rstd_made")
        h_made = sem("h_made")
        turned = sem("turned")
        turn_read = sem("turn_read")
        q_summed = sem("q_summed")
        q_made = sem("q_made")
        scores_summed = sem("scores_summed")
        scores_read = sem("scores_read")
        mask_step = sem("mask_step")
        max_made = sem("max_made")
        exp_made = sem("exp_made")
        probs_turned = sem("probs_turned")
        probs_read = sem("probs_read")
        ctx_summed = sem("ctx_summed")
        ctx_made = sem("ctx_made")
        out_summed = sem("out_summed")
        out_made = sem("out_made")
        out_stored = sem("out_stored")

        raw = {n: scores[:, i * C * D:(i + 1) * C * D].rearrange("p (k n) -> p k n", k=C)
               for i, n in enumerate(("wq", "wk"))}
        raw |= {n: adj_t[:, i * C * D:(i + 1) * C * D].rearrange("p (k n) -> p k n", k=C)
                for i, n in enumerate(("wv", "wmT"))}

        block = ctx.enter_context(nc.Block())

        @block.sync
        def _(sp):
            for name, src in (("wq", wq), ("wk", wk), ("wv", wv), ("wmT", wmT)):
                sp.dma_start(raw[name], src.rearrange("(k p) n -> p k n", p=P)).then_inc(weights_in, 16)
            for i, src in enumerate((bq, bk, bv)):
                sp.dma_start(bias_cols[:, i, :], src).then_inc(weights_in, 16)
            sp.dma_start(b_out[:, :], bm.partition_broadcast(P)).then_inc(weights_in, 16)
            sp.dma_start(keys_T[:, :, :], keyT.rearrange("(k p) n -> p k n", p=P)).then_inc(keys_in, 16)
            sp.dma_start(values[:, :, :], value.rearrange("(t p) n -> p t n", p=P)).then_inc(values_in, 16)
            sp.sem_inc(out_stored, 16)
            with sp.Fori(0, T) as t:
                row = sp.snap(t * P)
                sp.wait_ge(x_used, t + 1)
                sp.dma_start(x_t[:, :], x[bass.ds(row, P), :]).then_inc(x_in, 16)
                sp.wait_ge(adj_used, t + 1)
                sp.dma_start(adj_t[:, :], adj[bass.ds(row, P), :]).then_inc(adj_in, 16)
                sp.wait_ge(out_made, t + 1)
                sp.dma_start(out[bass.ds(row, P), :], out_t[:, :]).then_inc(out_stored, 16)
            sp.wait_ge(out_stored, 16 * T + 16)

        @block.gpsimd
        def _(pool):
            nc.gpsimd.memset(ident[:, :], 0.0).then_inc(zeros_made, 1)
            pool.wait_ge(zeros_made, 1)
            nc.gpsimd.affine_select(out=ident[:, :], in_=ident[:, :], compare_op=ALU.not_equal, fill=1.0,
                                    base=0, pattern=[[-1, P]], channel_multiplier=1).then_inc(consts_made, 1)
            nc.gpsimd.memset(ones[:, :], 1.0).then_inc(consts_made, 1)
            nc.gpsimd.memset(half[:, :], -0.5).then_inc(consts_made, 1)
            pool.wait_ge(consts_made, 3)
            with pool.Fori(0, T) as t:
                pool.wait_ge(stats_made, t + 1)
                nc.gpsimd.tensor_tensor(rstd[:, :], var_eps[:, :], half[:, :], ALU.pow).then_inc(rstd_made, 1)

        @block.scalar
        def _(act):
            act.wait_ge(weights_in, 16 * 8)
            act.wait_ge(consts_made, 3)
            for i, b in enumerate((0, 2)):
                for c in range(C):
                    nc.scalar.activation(bias_wide[:, i, c, :], ones[:, :], ACT.Copy,
                                         scale=bias_cols[:, b, c:c + 1]).then_inc(wide_made, 1)
            with act.Fori(0, T) as t:
                act.wait_ge(stats_made, t + 1)
                nc.scalar.activation(h_t[:, :], x_t[:, :], ACT.Relu, bias=neg_mean[:, :]).then_inc(h_made, 1)
                act.wait_ge(turned, 3 * t + 1)
                nc.scalar.copy(hT[:, :, :], p_turn[:, :].rearrange("p (c n) -> p c n", c=C)).then_inc(turn_read, 1)
                act.wait_ge(turned, 3 * t + 2)
                nc.scalar.copy(qT[:, :, :], p_turn[:, :].rearrange("p (c n) -> p c n", c=C)).then_inc(turn_read, 1)
                for j in range(J):
                    act.wait_ge(scores_summed, J * t + j + 1)
                    nc.scalar.activation(scores[:, j * W:(j + 1) * W], p_scores[j % 2][:, :], ACT.Identity,
                                         bias=shift_scaled[:, :], scale=INV).then_inc(scores_read, 1)
                act.wait_ge(max_made, t + 1)
                nc.scalar.activation(scores[:, :], scores[:, :], ACT.Exp, bias=neg_max[:, :],
                                     accum_out=row_sum[:, :]).then_inc(exp_made, 1)
                act.wait_ge(turned, 3 * t + 3)
                nc.scalar.copy(ctxT[:, :, :], p_turn[:, :].rearrange("p (c n) -> p c n", c=C)).then_inc(turn_read, 1)

        @block.vector
        def _(dve):
            dve.wait_ge(products, 1)
            nc.vector.tensor_copy(w_scores[:, 0, :], p_scores[0][:, :]).then_inc(products_read, 1)
            for n in range(1, 2 * C):
                dve.wait_ge(products, n + 1)
                to = w_scores[:, n, :] if n < C else w_out[:, n - C, :]
                nc.vector.tensor_copy(to, p_scores[n % 2][:, :]).then_inc(products_read, 1)
            dve.wait_ge(products, 2 * C + 1)
            nc.vector.tensor_copy(b_scores[:, :], p_probs[0][:, :]).then_inc(products_read, 1)
            dve.wait_ge(weights_in, 16 * 8)
            nc.vector.tensor_tensor(b_out[:, :], p_probs[1][:, :], b_out[:, :], ALU.add).then_inc(products_read, 1)
            nc.vector.tensor_copy(w_shift[:, :], p_shift[:, 0:C]).then_inc(products_read, 1)
            nc.vector.tensor_copy(b_shift[:, :], p_shift[:, C:C + 1]).then_inc(products_read, 1)
            dve.wait_ge(products_read, 2 * C + 4)
            nc.vector.tensor_copy(shift[:, :], b_shift[:, :]).then_inc(x_used, 1)
            nc.vector.tensor_copy(shift_scaled[:, :], b_shift[:, :]).then_inc(adj_used, 1)
            STATS, MASKS = 4, 4 * J + 1
            with dve.Fori(0, T) as t:
                dve.wait_ge(x_in, 16 * t + 16)
                nc.vector.bn_stats(stats[:, :], x_t[:, :]).then_inc(stats_step, 1)
                dve.wait_ge(stats_step, STATS * t + 1)
                nc.vector.tensor_copy(shift_scaled[:, :], stats[:, 1:2]).then_inc(stats_step, 1)
                nc.vector.bn_aggr(mean_var[:, :], stats[:, :]).then_inc(stats_step, 1)
                dve.wait_ge(stats_step, STATS * t + 3)
                nc.vector.tensor_scalar(neg_mean[:, :], mean_var[:, 0:1], -1.0, None, ALU.mult).then_inc(stats_step, 1)
                dve.wait_ge(stats_step, STATS * t + 4)
                nc.vector.tensor_scalar(var_eps[:, :], mean_var[:, 1:2], EPS, None, ALU.add).then_inc(stats_made, 1)
                dve.wait_ge(q_summed, t + 1)
                dve.wait_ge(rstd_made, t + 1)
                nc.vector.scalar_tensor_tensor(q_t[:, :], p_proj[:, :], rstd[:, :], b_scores[:, :],
                                               ALU.mult, ALU.add).then_inc(q_made, 1)
                nc.vector.scalar_tensor_tensor(shift[:, :], p_shift[:, 0:1], rstd[:, :], b_shift[:, :],
                                               ALU.mult, ALU.add).then_inc(q_made, 1)
                dve.wait_ge(q_made, 3 * t + 2)
                nc.vector.tensor_scalar(shift_scaled[:, :], shift[:, :], INV, None, ALU.mult).then_inc(q_made, 1)
                dve.wait_ge(adj_in, 16 * t + 16)
                for j in range(J):
                    own = scores[:, j * W:(j + 1) * W]
                    dve.wait_ge(scores_read, J * t + j + 1)
                    nc.vector.tensor_tensor(own, own, adj_t[:, j * W:(j + 1) * W], ALU.mult).then_inc(mask_step, 1)
                    dve.wait_ge(mask_step, MASKS * t + 4 * j + 1)
                    nc.vector.tensor_scalar(below[:, :], own, THRESHOLD, MASKED, ALU.is_lt, ALU.mult).then_inc(mask_step, 1)
                    dve.wait_ge(mask_step, MASKS * t + 4 * j + 2)
                    nc.vector.scalar_tensor_tensor(below[:, :], own, -THRESHOLD, below[:, :],
                                                   ALU.is_gt, ALU.mult).then_inc(mask_step, 1)
                    dve.wait_ge(mask_step, MASKS * t + 4 * j + 3)
                    nc.vector.tensor_tensor(own, own, below[:, :], ALU.add).then_inc(mask_step, 1)
                    if j == J - 1:
                        dve.wait_ge(mask_step, MASKS * t + 4 * J)
                        nc.vector.tensor_scalar(below[:, 0:1], shift[:, :], 1.0, None, ALU.mult).then_inc(adj_used, 1)
                nc.vector.reduce_max(row_max[:, :], scores[:, :], AX.X).then_inc(mask_step, 1)
                dve.wait_ge(mask_step, MASKS * t + MASKS)
                nc.vector.tensor_scalar(neg_max[:, :], row_max[:, :], -1.0, None, ALU.mult).then_inc(max_made, 1)
                for j in range(J):
                    dve.wait_ge(probs_turned, J * t + j + 1)
                    nc.vector.tensor_copy(probs_T[:, j % 2, :], p_probs[j % 2][:, :]).then_inc(probs_read, 1)
                dve.wait_ge(exp_made, t + 1)
                nc.vector.reciprocal(inv_sum[:, :], row_sum[:, :]).then_inc(ctx_made, 1)
                dve.wait_ge(ctx_made, 2 * t + 1)
                dve.wait_ge(ctx_summed, t + 1)
                nc.vector.tensor_scalar(ctx_t[:, :], p_ctx[:, :], inv_sum[:, :], None, ALU.mult).then_inc(ctx_made, 1)
                nc.vector.tensor_tensor(x_bias[:, :], x_t[:, :], b_out[:, :], ALU.add).then_inc(x_used, 1)
                dve.wait_ge(x_used, t + 2)
                dve.wait_ge(out_summed, t + 1)
                dve.wait_ge(out_stored, 16 * t + 16)
                nc.vector.tensor_tensor(out_t[:, :], p_proj[:, :], x_bias[:, :], ALU.add).then_inc(out_made, 1)

        @block.tensor
        def _(pe):
            pe.wait_ge(weights_in, 16 * 8)
            for n in range(2 * C):
                left, right = ("wq", "wk") if n < C else ("wv", "wmT")
                c = n % C
                if n >= 2:
                    pe.wait_ge(products_read, n - 1)
                for k in range(C):
                    last = nc.tensor.matmul(p_scores[n % 2][:, :], raw[left][:, k, c * P:(c + 1) * P],
                                            raw[right][:, k, :], start=(k == 0), stop=(k == C - 1))
                last.then_inc(products, 1)
            pe.wait_ge(wide_made, 2 * C)
            for i, right in enumerate(("wk", "wmT")):
                for k in range(C):
                    nc.tensor.matmul(p_probs[i][:, :], bias_wide[:, i, k, :], raw[right][:, k, :],
                                     start=(k == 0), stop=(k == C - 1))
            for c in range(C):
                for k in range(C):
                    nc.tensor.matmul(p_shift[:, c:c + 1], raw["wq"][:, k, c * P:(c + 1) * P],
                                     bias_cols[:, 1, k:k + 1], start=(k == 0), stop=(k == C - 1))
            for k in range(C):
                last = nc.tensor.matmul(p_shift[:, C:C + 1], bias_wide[:, 0, k, :], bias_cols[:, 1, k:k + 1],
                                        start=(k == 0), stop=(k == C - 1))
            last.then_inc(products, 1)
            pe.wait_ge(products_read, 2 * C + 4)
            pe.wait_ge(keys_in, 16)
            pe.wait_ge(values_in, 16)
            pe.wait_ge(consts_made, 3)
            with pe.Fori(0, T) as t:
                pe.wait_ge(h_made, t + 1)
                for c in range(C):
                    last = nc.tensor.transpose(p_turn[:, c * P:(c + 1) * P], h_t[:, c * P:(c + 1) * P], ident[:, :])
                last.then_inc(turned, 1)
                pe.wait_ge(turn_read, 3 * t + 1)
                for c in range(C):
                    nc.tensor.matmul(p_proj[:, :], hT[:, c, :], w_scores[:, c, :], start=(c == 0), stop=(c == C - 1))
                for c in range(C):
                    last = nc.tensor.matmul(p_shift[:, 0:1], hT[:, c, :], w_shift[:, c:c + 1],
                                            start=(c == 0), stop=(c == C - 1))
                last.then_inc(q_summed, 1)
                pe.wait_ge(q_made, 3 * t + 3)
                for c in range(C):
                    last = nc.tensor.transpose(p_turn[:, c * P:(c + 1) * P], q_t[:, c * P:(c + 1) * P], ident[:, :])
                last.then_inc(turned, 1)
                pe.wait_ge(turn_read, 3 * t + 2)
                for j in range(J):
                    if j >= 2:
                        pe.wait_ge(scores_read, J * t + j - 1)
                    for c in range(C):
                        last = nc.tensor.matmul(p_scores[j % 2][:, :], qT[:, c, :], keys_T[:, c, j * W:(j + 1) * W],
                                                start=(c == 0), stop=(c == C - 1))
                    last.then_inc(scores_summed, 1)
                pe.wait_ge(exp_made, t + 1)

                def turn_probs(j):
                    if j >= 2:
                        pe.wait_ge(probs_read, J * t + j - 1)
                    for g in range(G):
                        at = j * W + g * P
                        last = nc.tensor.transpose(p_probs[j % 2][:, g * P:(g + 1) * P], scores[:, at:at + P], ident[:, :])
                    last.then_inc(probs_turned, 1)

                turn_probs(0)
                for j in range(J):
                    if j + 1 < J:
                        turn_probs(j + 1)
                    pe.wait_ge(probs_read, J * t + j + 1)
                    for g in range(G):
                        last = nc.tensor.matmul(p_ctx[:, :], probs_T[:, j % 2, g * P:(g + 1) * P],
                                                values[:, j * G + g, :],
                                                start=(j == 0 and g == 0), stop=(j == J - 1 and g == G - 1))
                last.then_inc(ctx_summed, 1)
                pe.wait_ge(ctx_made, 2 * t + 2)
                for c in range(C):
                    last = nc.tensor.transpose(p_turn[:, c * P:(c + 1) * P], ctx_t[:, c * P:(c + 1) * P], ident[:, :])
                last.then_inc(turned, 1)
                pe.wait_ge(turn_read, 3 * t + 3)
                for c in range(C):
                    last = nc.tensor.matmul(p_proj[:, :], ctxT[:, c, :], w_out[:, c, :], start=(c == 0), stop=(c == C - 1))
                last.then_inc(out_summed, 1)


def kernel(**inputs):
    import numpy as np
    import concourse.bacc as bacc
    from concourse.bass_utils import run_bass_kernel_spmd

    def down(b):
        return np.ascontiguousarray(b.reshape(-1, P).T)

    g = {n.removeprefix("L0_gnn_"): np.asarray(a) for n, a in inputs.items()}
    laid = {
        "x": g["x"], "adj": g["adj"], "keyT": g["key"].T, "value": g["value"],
        "wq": g["Wq"], "wk": g["Wk"], "wv": g["Wv"], "wmT": g["Wm"].T,
        "bq": down(g["bq"]), "bk": down(g["bk"]), "bv": down(g["bv"]), "bm": g["bm"],
    }
    nc = bacc.Bacc("TRN2", target_bir_lowering=False, num_devices=1)
    arrays, args = {}, {}
    for name, a in laid.items():
        a = np.ascontiguousarray(a)
        arrays[f"in_{name}"] = a
        args[name] = nc.dram_tensor(f"in_{name}", a.shape, mybir.dt.from_np(a.dtype), kind="ExternalInput").ap()
    shape = g["x"].shape
    args["out"] = nc.dram_tensor("out_0", shape, F32, kind="ExternalOutput").ap()
    graph_attention(nc, **args)
    r = run_bass_kernel_spmd(nc, [arrays], core_ids=[0])
    return r.results[0]["out_0"]
```

```python
from contextlib import ExitStack

import concourse.bass as bass
from concourse import mybir

F32 = mybir.dt.float32
BF16 = mybir.dt.bfloat16
U32 = mybir.dt.uint32
I32 = mybir.dt.int32
ALU = mybir.AluOpType
ACT = mybir.ActivationFunctionType
AX = mybir.AxisListType
P = 128
MASKED = -1e9
THRESHOLD = 1e-5
EPS = 1e-5
TOP = 8
SLOTS = TOP
REST = 2 * TOP
FAR = 1000


def graph_attention(nc, x, adj, keyT, kv, wq, wk, wv, wmT, bq, bk, bv, bm, records, out):
    N, D = x.shape
    T = N // P
    C = D // P
    W = 512
    J = N // W
    G = W // P
    INV = 1.0 / float(N) ** 0.5
    STAGED = 8
    SCAN = 2 * J + 8
    DOTS = SLOTS + 8
    assert N % (2 * P) == 0 and D == W and J * TOP == 64

    with ExitStack() as ctx:
        def sb(name, shape, dt=F32):
            return ctx.enter_context(nc.sbuf_tensor(name, shape, dt))

        def sem(name):
            return ctx.enter_context(nc.semaphore(name))

        w_scores = sb("w_scores", [P, C, D])
        w_out = sb("w_out", [P, C, D])
        w_shift = sb("w_shift", [P, C])
        b_scores = sb("b_scores", [P, D])
        b_out = sb("b_out", [P, D])
        b_shift = sb("b_shift", [P, 1])
        ident = sb("ident", [P, P])
        ones = sb("ones", [P, P])
        bias_cols = sb("bias_cols", [P, 3, C])
        half = sb("half", [P, 1])

        keys_T = sb("keys_T", [P, C, N])
        values = sb("values", [P, T, D])
        scores = sb("scores", [P, N])
        adj_t = sb("adj_t", [P, N])

        edges_kv = keys_T[:, :, :].rearrange("p c n -> p (c n)").rearrange("p (s n) -> p s n", n=2 * D)
        edges = [edges_kv[:, b * SLOTS:(b + 1) * SLOTS, :] for b in range(2)]
        raw_flat = keys_T[:, :, :].rearrange("p c n -> p (c n)")[:, 2 * D * SLOTS:]
        raw = {n: raw_flat[:, i * C * D:(i + 1) * C * D].rearrange("p (k n) -> p k n", k=C)
               for i, n in enumerate(("wq", "wk", "wv", "wmT"))}
        values_flat = values[:, :, :].rearrange("p t n -> p (t n)")
        mask = [values_flat[:, b * N:(b + 1) * N] for b in range(2)]
        staged = [values_flat[:, (2 + b) * N:(3 + b) * N].rearrange("p (t n) -> p t n", t=STAGED) for b in range(2)]
        flags_bf16 = scores[:, 0:T * J * TOP].bitcast(BF16).rearrange("p (k t n) -> p k t n", k=2, t=T)
        odd_all = flags_bf16[:, 0]
        more_all = flags_bf16[:, 1]
        product = [scores[:, T * J * TOP + b * D:T * J * TOP + (b + 1) * D] for b in range(2)]
        value_sum = scores[:, T * J * TOP + 2 * D:T * J * TOP + 3 * D]
        relu_junk = adj_t[:, 0:N // 2].bitcast(BF16)
        diag = adj_t[:, N // 2:N // 2 + REST * P].rearrange("p (s n) -> p s n", s=REST)

        x_t = [sb(f"x_t{b}", [P, D]) for b in range(2)]
        x_bias = [sb(f"x_bias{b}", [P, D]) for b in range(2)]
        out_t = [sb(f"out_t{b}", [P, D]) for b in range(2)]
        stats = sb("stats", [P, 6])
        mean_var = sb("mean_var", [P, 2])
        var_eps = sb("var_eps", [P, 1])
        rstd = sb("rstd", [P, 1])
        neg_mean = sb("neg_mean", [P, 1])
        h_t = sb("h_t", [P, D])
        hT = sb("hT", [P, C, P])
        q_t = sb("q_t", [P, D])
        shift = sb("shift", [P, 1])
        shift_scaled = sb("shift_scaled", [P, 1])
        ctx_t = sb("ctx_t", [P, D])
        ctxT = sb("ctxT", [P, C, P])

        cand = sb("cand", [P, J, TOP])
        where = sb("where", [P, J, TOP], U32)
        group_top = sb("group_top", [P, J, TOP])
        expected = sb("expected", [P, J, TOP])
        is_expected = sb("is_expected", [P, J, TOP])
        key_of = sb("key_of", [P, J, TOP])
        edge_key = sb("edge_key", [P, J, TOP])
        later_key = sb("later_key", [P, J, TOP])
        top_key = sb("top_key", [P, REST])
        record = [sb(f"record{b}", [P, REST + 1], U32) for b in range(2)]
        used = [sb(f"used{b}", [P, REST]) for b in range(2)]
        row_numbers = sb("row_numbers", [P, T], U32)
        place_of = [sb(f"place_of{b}", [P, 1], U32) for b in range(2)]
        before = sb("before", [P, P])
        flagged = sb("flagged", [P, 1])
        blank = sb("blank", [P, REST + 1], U32)
        negatives = sb("negatives", [P, T])
        dots = sb("dots", [P, REST])
        scaled = sb("scaled", [P, REST])
        low = sb("low", [P, REST])
        masked = [sb("masked", [P, SLOTS + 1]), sb("masked_rest", [P, REST + 1])]
        row_max = sb("row_max", [P, 1])
        neg_max = sb("neg_max", [P, 1])
        e_t = [sb("e_t", [P, SLOTS + 1]), sb("e_rest", [P, REST + 1])]
        weight = sb("weight", [P, REST])
        weight_sum = sb("weight_sum", [P, 1])
        row_sum = sb("row_sum", [P, 1])
        inv_sum = sb("inv_sum", [P, 1])
        verdict = sb("verdict", [P, 8])
        verdict_i = sb("verdict_i", [P, 1], I32)

        bank = [ctx.enter_context(nc.psum_tensor(f"bank{i}", [P, W], F32)) for i in range(8)]
        p_turn, p_proj, p_shift, p_place, p_ctx, p_out, p_turn_ctx, p_spare = bank
        p_weights = [p_place, p_out, p_turn_ctx, p_spare]

        weights_in = sem("weights_in")
        late_weights_in = sem("late_weights_in")
        zeros_made = sem("zeros_made")
        consts_made = sem("consts_made")
        wide_made = sem("wide_made")
        products = sem("products")
        products_read = sem("products_read")
        bias_done = sem("bias_done")
        staged_in = [sem(f"staged_in{b}") for b in range(2)]
        staged_used = sem("staged_used")
        blank_in = sem("blank_in")
        x_in = [sem(f"x_in{b}") for b in range(2)]
        mask_in = [sem(f"mask_in{b}") for b in range(2)]
        stats_step = sem("stats_step")
        stats_made = sem("stats_made")
        rstd_made = sem("rstd_made")
        h_made = sem("h_made")
        h_turned = sem("h_turned")
        hT_made = sem("hT_made")
        q_summed = sem("q_summed")
        q_made = sem("q_made")
        scan_step = sem("scan_step")
        mask_scanned = sem("mask_scanned")
        mask_checked = sem("mask_checked")
        columns_made = sem("columns_made")
        used_made = sem("used_made")
        place_summed = sem("place_summed")
        place_made = sem("place_made")
        flagged_made = sem("flagged_made")
        recorded = [sem(f"recorded{b}") for b in range(2)]
        edges_in = [sem(f"edges_in{b}") for b in range(2)]
        dot_step = sem("dot_step")
        max_made = sem("max_made")
        exp_made = sem("exp_made")
        weights_made = sem("weights_made")
        diag_made = sem("diag_made")
        ctx_summed = sem("ctx_summed")
        ctx_made = sem("ctx_made")
        ctx_turned = sem("ctx_turned")
        ctxT_made = sem("ctxT_made")
        out_summed = sem("out_summed")
        x_bias_made = sem("x_bias_made")
        out_made = sem("out_made")
        out_stored = [sem(f"out_stored{b}") for b in range(2)]
        rest_listed = sem("rest_listed")
        rest_in = sem("rest_in")
        rest_used = sem("rest_used")
        rest_stored = sem("rest_stored")
        verdict_step = sem("verdict_step")
        verdict_summed = sem("verdict_summed")
        verdict_made = sem("verdict_made")

        below = out_t[1]
        d_probs_T = x_t[1], x_bias[1]
        d_names = ("keys_in values_in x_in adj_in x_used adj_used stats_step stats_made rstd_made h_made turned "
                   "turn_read q_summed q_made scores_summed scores_read mask_step max_made exp_made probs_turned "
                   "probs_read ctx_summed ctx_made out_summed out_made out_stored").split()
        d = {name: sem(f"d_{name}") for name in d_names}
        p_scores, p_probs = (p_place, p_out), (p_turn_ctx, p_spare)

        def if_dense(eng):
            eng.wait_ge(verdict_made, 1)
            return eng.If(eng.value_load(verdict_i[0:1, 0:1], min_val=0, max_val=1) < 1)

        def dense_sync(sp):
            with if_dense(sp):
                sp.dma_start(keys_T[:, :, :], keyT.rearrange("(k p) n -> p k n", p=P)).then_inc(d["keys_in"], 16)
                sp.dma_start(values[:, :, :], kv[:, D:2 * D].rearrange("(t p) n -> p t n", p=P)).then_inc(d["values_in"], 16)
                sp.sem_inc(d["out_stored"], 16)
                with sp.Fori(0, T) as t:
                    row = sp.snap(t * P)
                    sp.wait_ge(d["x_used"], t + 1)
                    sp.dma_start(x_t[0][:, :], x[bass.ds(row, P), :]).then_inc(d["x_in"], 16)
                    sp.wait_ge(d["adj_used"], t + 1)
                    sp.dma_start(adj_t[:, :], adj[bass.ds(row, P), :]).then_inc(d["adj_in"], 16)
                    sp.wait_ge(d["out_made"], t + 1)
                    sp.dma_start(out[bass.ds(row, P), :], out_t[0][:, :]).then_inc(d["out_stored"], 16)
                sp.wait_ge(d["out_stored"], 16 * T + 16)

        def dense_gpsimd(pool):
            with if_dense(pool), pool.Fori(0, T) as t:
                pool.wait_ge(d["stats_made"], t + 1)
                nc.gpsimd.tensor_tensor(rstd[:, :], var_eps[:, :], half[:, :], ALU.pow).then_inc(d["rstd_made"], 1)

        def dense_scalar(act):
            def read_turned(to, n):
                act.wait_ge(d["turned"], n)
                nc.scalar.copy(to[:, :, :], p_turn[:, :].rearrange("p (c n) -> p c n", c=C)).then_inc(d["turn_read"], 1)

            with if_dense(act), act.Fori(0, T) as t:
                act.wait_ge(d["stats_made"], t + 1)
                nc.scalar.activation(h_t[:, :], x_t[0][:, :], ACT.Relu, bias=neg_mean[:, :]).then_inc(d["h_made"], 1)
                read_turned(hT, 3 * t + 1)
                read_turned(ctxT, 3 * t + 2)
                for j in range(J):
                    act.wait_ge(d["scores_summed"], J * t + j + 1)
                    nc.scalar.activation(scores[:, j * W:(j + 1) * W], p_scores[j % 2][:, :], ACT.Identity,
                                         bias=shift_scaled[:, :], scale=INV).then_inc(d["scores_read"], 1)
                act.wait_ge(d["max_made"], t + 1)
                nc.scalar.activation(scores[:, :], scores[:, :], ACT.Exp, bias=neg_max[:, :],
                                     accum_out=row_sum[:, :]).then_inc(d["exp_made"], 1)
                read_turned(ctxT, 3 * t + 3)

        def dense_vector(dve):
            STATS, MASKS = 3, 4 * J + 1
            with if_dense(dve):
                dve.sem_inc(d["x_used"], 1)
                dve.sem_inc(d["adj_used"], 1)
                with dve.Fori(0, T) as t:
                    alone(dve, (d["x_in"], 16 * t + 16))
                    nc.vector.bn_stats(stats[:, :], x_t[0][:, :]).then_inc(d["stats_step"], 1)
                    alone(dve, (d["stats_step"], STATS * t + 1))
                    nc.vector.bn_aggr(mean_var[:, :], stats[:, :]).then_inc(d["stats_step"], 1)
                    dve.wait_ge(d["stats_step"], STATS * t + 2)
                    nc.vector.tensor_scalar(neg_mean[:, :], mean_var[:, 0:1], -1.0, None, ALU.mult).then_inc(d["stats_step"], 1)
                    nc.vector.tensor_scalar(var_eps[:, :], mean_var[:, 1:2], EPS, None, ALU.add).then_inc(d["stats_made"], 1)
                    dve.wait_ge(d["q_summed"], t + 1)
                    dve.wait_ge(d["rstd_made"], t + 1)
                    nc.vector.scalar_tensor_tensor(q_t[:, :], p_proj[:, :], rstd[:, :], b_scores[:, :],
                                                   ALU.mult, ALU.add).then_inc(d["q_made"], 1)
                    nc.vector.scalar_tensor_tensor(shift[:, :], p_shift[:, 0:1], rstd[:, :], b_shift[:, :],
                                                   ALU.mult, ALU.add).then_inc(d["q_made"], 1)
                    dve.wait_ge(d["q_made"], 3 * t + 2)
                    nc.vector.tensor_scalar(shift_scaled[:, :], shift[:, :], INV, None, ALU.mult).then_inc(d["q_made"], 1)
                    dve.wait_ge(d["adj_in"], 16 * t + 16)
                    for j in range(J):
                        own = scores[:, j * W:(j + 1) * W]
                        n = MASKS * t + 4 * j
                        dve.wait_ge(d["scores_read"], J * t + j + 1)
                        nc.vector.tensor_tensor(own, own, adj_t[:, j * W:(j + 1) * W], ALU.mult).then_inc(d["mask_step"], 1)
                        dve.wait_ge(d["mask_step"], n + 1)
                        nc.vector.tensor_scalar(below[:, :], own, THRESHOLD, MASKED, ALU.is_lt, ALU.mult).then_inc(d["mask_step"], 1)
                        dve.wait_ge(d["mask_step"], n + 2)
                        nc.vector.scalar_tensor_tensor(below[:, :], own, -THRESHOLD, below[:, :],
                                                       ALU.is_gt, ALU.mult).then_inc(d["mask_step"], 1)
                        dve.wait_ge(d["mask_step"], n + 3)
                        nc.vector.tensor_tensor(own, own, below[:, :], ALU.add).then_inc(d["mask_step"], 1)
                    dve.wait_ge(d["mask_step"], MASKS * t + 4 * J)
                    nc.vector.tensor_scalar(mean_var[:, 0:1], shift[:, :], 1.0, None, ALU.mult).then_inc(d["adj_used"], 1)
                    nc.vector.reduce_max(row_max[:, :], scores[:, :], AX.X).then_inc(d["mask_step"], 1)
                    dve.wait_ge(d["mask_step"], MASKS * t + MASKS)
                    nc.vector.tensor_scalar(neg_max[:, :], row_max[:, :], -1.0, None, ALU.mult).then_inc(d["max_made"], 1)
                    for j in range(J):
                        dve.wait_ge(d["probs_turned"], J * t + j + 1)
                        nc.vector.tensor_copy(d_probs_T[j % 2][:, :], p_probs[j % 2][:, :]).then_inc(d["probs_read"], 1)
                    dve.wait_ge(d["exp_made"], t + 1)
                    nc.vector.reciprocal(inv_sum[:, :], row_sum[:, :]).then_inc(d["ctx_made"], 1)
                    dve.wait_ge(d["ctx_made"], 2 * t + 1)
                    dve.wait_ge(d["ctx_summed"], t + 1)
                    nc.vector.tensor_scalar(ctx_t[:, :], p_ctx[:, :], inv_sum[:, :], None, ALU.mult).then_inc(d["ctx_made"], 1)
                    nc.vector.tensor_tensor(x_bias[0][:, :], x_t[0][:, :], b_out[:, :], ALU.add).then_inc(d["x_used"], 1)
                    dve.wait_ge(d["x_used"], t + 2)
                    dve.wait_ge(d["out_summed"], t + 1)
                    dve.wait_ge(d["out_stored"], 16 * t + 16)
                    nc.vector.tensor_tensor(out_t[0][:, :], p_proj[:, :], x_bias[0][:, :], ALU.add).then_inc(d["out_made"], 1)

        def dense_tensor(pe):
            def turn(source, into, count):
                for c in range(C):
                    last = nc.tensor.transpose(into[:, c * P:(c + 1) * P], source[:, c * P:(c + 1) * P], ident[:, :])
                last.then_inc(count, 1)

            with if_dense(pe):
                pe.wait_ge(d["keys_in"], 16)
                pe.wait_ge(d["values_in"], 16)
                with pe.Fori(0, T) as t:
                    pe.wait_ge(d["h_made"], t + 1)
                    turn(h_t, p_turn, d["turned"])
                    pe.wait_ge(d["turn_read"], 3 * t + 1)
                    for c in range(C):
                        nc.tensor.matmul(p_proj[:, :], hT[:, c, :], w_scores[:, c, :], start=(c == 0), stop=(c == C - 1))
                    for c in range(C):
                        last = nc.tensor.matmul(p_shift[:, 0:1], hT[:, c, :], w_shift[:, c:c + 1],
                                                start=(c == 0), stop=(c == C - 1))
                    last.then_inc(d["q_summed"], 1)
                    pe.wait_ge(d["q_made"], 3 * t + 3)
                    turn(q_t, p_turn, d["turned"])
                    pe.wait_ge(d["turn_read"], 3 * t + 2)
                    for j in range(J):
                        if j >= 2:
                            pe.wait_ge(d["scores_read"], J * t + j - 1)
                        for c in range(C):
                            last = nc.tensor.matmul(p_scores[j % 2][:, :], ctxT[:, c, :], keys_T[:, c, j * W:(j + 1) * W],
                                                    start=(c == 0), stop=(c == C - 1))
                        last.then_inc(d["scores_summed"], 1)
                    pe.wait_ge(d["exp_made"], t + 1)
                    turn(scores[:, 0:W], p_probs[0], d["probs_turned"])
                    for j in range(J):
                        if j + 1 < J:
                            if j >= 1:
                                pe.wait_ge(d["probs_read"], J * t + j)
                            turn(scores[:, (j + 1) * W:(j + 2) * W], p_probs[(j + 1) % 2], d["probs_turned"])
                        pe.wait_ge(d["probs_read"], J * t + j + 1)
                        for g in range(G):
                            last = nc.tensor.matmul(p_ctx[:, :], d_probs_T[j % 2][:, g * P:(g + 1) * P],
                                                    values[:, j * G + g, :],
                                                    start=(j == 0 and g == 0), stop=(j == J - 1 and g == G - 1))
                    last.then_inc(d["ctx_summed"], 1)
                    pe.wait_ge(d["ctx_made"], 2 * t + 2)
                    turn(ctx_t, p_turn, d["turned"])
                    pe.wait_ge(d["turn_read"], 3 * t + 3)
                    for c in range(C):
                        last = nc.tensor.matmul(p_proj[:, :], ctxT[:, c, :], w_out[:, c, :], start=(c == 0), stop=(c == C - 1))
                    last.then_inc(d["out_summed"], 1)

        block = ctx.enter_context(nc.Block())
        LAST = T - 1
        PRODUCTS = 2 * C + 4

        def alone(eng, *waits):
            waits = [(semaphore, value if isinstance(value, int) else eng.to_reg(value)) for semaphore, value in waits]
            eng.wait_ge(consts_made, 1)
            for semaphore, value in waits:
                eng.wait_ge(semaphore, value)

        @block.sync
        def _(sp):
            def load_x(t, b):
                sp.dma_start(x_t[b][:, :], x[bass.ts(t, P), :]).then_inc(x_in[b], 16)

            def load_mask(t, b):
                sp.dma_start(mask[b], adj[bass.ts(t, P), :]).then_inc(mask_in[b], 16)

            load_x(0, 0)
            load_mask(0, 0)
            for name, src in (("wq", wq), ("wk", wk)):
                sp.dma_start(raw[name], src.rearrange("(k p) n -> p k n", p=P)).then_inc(weights_in, 16)
            for i, src in enumerate((bq, bk, bv)):
                sp.dma_start(bias_cols[:, i, :], src).then_inc(weights_in, 16)
            load_x(1, 1)
            load_mask(1, 1)
            for name, src in (("wv", wv), ("wmT", wmT)):
                sp.dma_start(raw[name], src.rearrange("(k p) n -> p k n", p=P)).then_inc(late_weights_in, 16)
            sp.dma_start(x_bias[1][:, :], bm.partition_broadcast(P)).then_inc(late_weights_in, 16)
            for s in range(T // STAGED):
                if s >= 2:
                    sp.wait_ge(staged_used, s - 1)
                src = kv[s * STAGED * P:(s + 1) * STAGED * P, D:2 * D].rearrange("(t p) n -> p t n", p=P)
                sp.dma_start(staged[s % 2], src).then_inc(staged_in[s % 2], 16)
            sp.wait_ge(consts_made, 1)
            sp.dma_start(records, blank[:, :]).then_inc(blank_in, 16)
            for b in range(2):
                sp.sem_inc(out_stored[b], 16)

            def loads(t, b):
                sp.wait_ge(mask_scanned, t - 1)
                sp.wait_ge(mask_checked, t - 1)
                load_mask(t, b)
                sp.wait_ge(x_bias_made, t - 1)
                load_x(t, b)

            def store(t, b):
                sp.wait_ge(out_made, t + 1)
                sp.dma_start(out[bass.ts(t, P), :], out_t[b][:, :]).then_inc(out_stored[b], 16)

            for t in (2, 3):
                loads(t, t % 2)
            with sp.Fori(2, T // 2) as u:
                for b in range(2):
                    loads(2 * u + b, b)
                    store(2 * u + b - 4, b)
            for t in range(T - 4, T):
                store(t, t % 2)
            for b in range(2):
                sp.wait_ge(recorded[b], 16 * (T // 2))
            sp.dma_start(record[0][:, :], records).then_inc(rest_listed, 16)
            for b in range(2):
                sp.wait_ge(out_stored[b], 16 * (T // 2) + 16)
            sp.wait_ge(rest_stored, 16)
            dense_sync(sp)

        @block.gpsimd
        def _(pool):
            for tile, value in ((ident, 0.0), (ones, 1.0), (before, 1.0), (half, -0.5), (expected, 1.0),
                                (flagged, 0.0), (masked[0], MASKED), (masked[1], MASKED)):
                nc.gpsimd.memset(tile[:], value).then_inc(zeros_made, 1)
            for g in range(J):
                nc.gpsimd.memset(group_top[:, g, :], float(N - g * W)).then_inc(zeros_made, 1)
            nc.gpsimd.iota(row_numbers[:, :], pattern=[[P, T]], base=0, channel_multiplier=1).then_inc(zeros_made, 1)
            nc.gpsimd.iota(blank[:, :], pattern=[[0, REST + 1]], base=N, channel_multiplier=0).then_inc(zeros_made, 1)
            pool.wait_ge(zeros_made, 8 + J + 2)
            nc.gpsimd.memset(expected[:, :, TOP - 1:TOP], 2.0).then_inc(zeros_made, 1)
            nc.gpsimd.affine_select(out=ident[:, :], in_=ident[:, :], compare_op=ALU.not_equal, fill=1.0,
                                    base=0, pattern=[[-1, P]], channel_multiplier=1).then_inc(zeros_made, 1)
            nc.gpsimd.affine_select(out=before[:, :], in_=before[:, :], compare_op=ALU.is_gt, fill=0.0,
                                    base=0, pattern=[[1, P]], channel_multiplier=-1).then_inc(zeros_made, 1)
            pool.wait_ge(zeros_made, 8 + J + 5)
            nc.gpsimd.affine_select(out=before[:, :], in_=before[:, :], compare_op=ALU.not_equal, fill=-float(FAR),
                                    base=0, pattern=[[1, P]], channel_multiplier=-1).then_inc(zeros_made, 1)
            pool.wait_ge(zeros_made, 8 + J + 6)
            nc.gpsimd.memset(half[:, :], -0.5).then_inc(consts_made, 1)
            nc.gpsimd.memset(edges[0], 0.0).then_inc(zeros_made, 1)

            def make_rstd(t):
                pool.wait_ge(stats_made, t + 1)
                nc.gpsimd.tensor_tensor(rstd[:, :], var_eps[:, :], half[:, :], ALU.pow).then_inc(rstd_made, 1)

            def gather(t, b, *free):
                alone(pool, (columns_made, t + 1), *free)
                for s in range(SLOTS):
                    nc.gpsimd.indirect_dma_start(
                        out=edges[b][:, s, :], out_offset=None, in_=kv,
                        in_offset=bass.IndirectOffsetOnAxis(ap=record[b][:, s:s + 1], axis=0),
                        bounds_check=N - 1, oob_is_err=False).then_inc(edges_in[b], 16)

            def add_bias(t, b):
                nc.gpsimd.tensor_tensor(x_bias[b][:, :], x_t[b][:, :], b_out[:, :], ALU.add).then_inc(x_bias_made, 1)

            def note(t, b):
                alone(pool, (place_made, t + 1))
                nc.gpsimd.indirect_dma_start(
                    out=records, out_offset=bass.IndirectOffsetOnAxis(ap=place_of[b][:, :], axis=0),
                    in_=record[b][:, :], in_offset=None,
                    bounds_check=P - 1, oob_is_err=False).then_inc(recorded[b], 16)

            make_rstd(0)
            pool.wait_ge(zeros_made, 8 + J + 7)
            gather(0, 0)
            make_rstd(1)
            pool.wait_ge(products_read, PRODUCTS)
            gather(1, 1)
            pool.wait_ge(late_weights_in, 48)
            nc.gpsimd.tensor_tensor(b_out[:, :], b_out[:, :], x_bias[1][:, :], ALU.add).then_inc(bias_done, 1)
            pool.wait_ge(bias_done, 1)
            add_bias(0, 0)
            pool.wait_ge(blank_in, 16)
            note(0, 0)
            note(1, 1)

            def step(t, b):
                make_rstd(t + 1)
                gather(t + 1, 1 - b, (ctx_summed, t))
                add_bias(t, b)
                note(t + 1, 1 - b)

            with pool.Fori(1, LAST, 2) as t:
                step(t, 1)
                step(t + 1, 0)
            pool.wait_ge(ctx_summed, LAST)
            add_bias(LAST, LAST % 2)
            pool.wait_ge(rest_listed, 16)
            pool.wait_ge(ctx_summed, T)
            nc.gpsimd.indirect_dma_start(
                out=x_t[0][:, :], out_offset=None, in_=x,
                in_offset=bass.IndirectOffsetOnAxis(ap=record[0][:, REST:REST + 1], axis=0),
                bounds_check=N - 1, oob_is_err=False).then_inc(rest_in, 16)
            for s in range(REST):
                nc.gpsimd.indirect_dma_start(
                    out=edges_kv[:, s, :], out_offset=None, in_=kv,
                    in_offset=bass.IndirectOffsetOnAxis(ap=record[0][:, s:s + 1], axis=0),
                    bounds_check=N - 1, oob_is_err=False).then_inc(edges_in[0], 16)
            make_rstd(T)
            pool.wait_ge(out_made, LAST)
            pool.wait_ge(rest_in, 16)
            add_bias(T, 0)
            pool.wait_ge(out_made, T + 1)
            for b in range(2):
                pool.wait_ge(out_stored[b], 16 * (T // 2) + 16)
            nc.gpsimd.indirect_dma_start(
                out=out, out_offset=bass.IndirectOffsetOnAxis(ap=record[0][:, REST:REST + 1], axis=0),
                in_=out_t[0][:, :], in_offset=None,
                bounds_check=N - 1, oob_is_err=False).then_inc(rest_stored, 16)
            pool.wait_ge(rest_stored, 16)
            dense_gpsimd(pool)

        @block.scalar
        def _(act):
            def relu(t, b):
                act.wait_ge(stats_made, t + 1)
                nc.scalar.activation(h_t[:, :], x_t[b][:, :], ACT.Relu, bias=neg_mean[:, :]).then_inc(h_made, 1)
                act.wait_ge(h_turned, t + 1)
                nc.scalar.copy(hT[:, :, :], p_turn[:, :].rearrange("p (c n) -> p c n", c=C)).then_inc(hT_made, 1)

            def check_mask(u, b):
                act.wait_ge(mask_in[b], 16 * u + 16)
                nc.scalar.activation(relu_junk, mask[b], ACT.Relu, scale=-1.0,
                                     accum_out=negatives[:, bass.ds(2 * u + b, 1)]).then_inc(mask_checked, 1)

            def read_ctx(t):
                act.wait_ge(ctx_turned, t + 1)
                nc.scalar.copy(ctxT[:, :, :], p_turn_ctx[:, :].rearrange("p (c n) -> p c n", c=C)).then_inc(ctxT_made, 1)

            def exponentials(t, masked_t, e):
                act.wait_ge(max_made, t + 1)
                nc.scalar.activation(e[:, :], masked_t[:, :], ACT.Exp, bias=neg_max[:, :]).then_inc(exp_made, 1)

            def diagonals(t, slots, first):
                act.wait_ge(weights_made, t + 1)
                if not first:
                    act.wait_ge(ctx_summed, t)
                for s in range(slots):
                    last = nc.scalar.activation(diag[:, s, :], ident[:, :], ACT.Copy, scale=weight[:, s:s + 1])
                last.then_inc(diag_made, 1)

            act.wait_ge(weights_in, 16 * 5)
            act.wait_ge(consts_made, 1)
            wide = [out_t[0], out_t[1]]
            for i, b in enumerate((0, 2)):
                for c in range(C):
                    nc.scalar.activation(wide[i][:, c * P:(c + 1) * P], ones[:, :], ACT.Copy,
                                         scale=bias_cols[:, b, c:c + 1]).then_inc(wide_made, 1)
            for c in range(C):
                act.wait_ge(products, c + 1)
                nc.scalar.copy(w_scores[:, c, :], p_weights[c][:, :]).then_inc(products_read, 1)
            act.wait_ge(products, C + 1)
            nc.scalar.copy(b_scores[:, :], p_ctx[:, :]).then_inc(products_read, 1)
            nc.scalar.copy(w_shift[:, :], p_shift[:, 0:C])
            nc.scalar.copy(b_shift[:, :], p_shift[:, C:C + 1]).then_inc(products_read, 1)
            relu(0, 0)
            check_mask(0, 0)
            for c in range(C):
                act.wait_ge(products, C + 2 + c)
                nc.scalar.copy(w_out[:, c, :], p_weights[c][:, :]).then_inc(products_read, 1)
            act.wait_ge(products, 2 * C + 2)
            nc.scalar.copy(b_out[:, :], p_ctx[:, :]).then_inc(products_read, 1)
            act.wait_ge(products, 2 * C + 3)
            nc.scalar.copy(value_sum, p_ctx[:, :]).then_inc(products_read, 1)
            relu(1, 1)
            check_mask(0, 1)
            exponentials(0, masked[0], e_t[0])
            diagonals(0, SLOTS, True)

            def step(u, b):
                t = 2 * u + b
                relu(t + 1, 1 - b)
                check_mask(u + b, 1 - b)
                read_ctx(t - 1)
                exponentials(t, masked[0], e_t[0])
                diagonals(t, SLOTS, False)

            with act.Fori(0, LAST // 2) as u:
                step(u, 1)
                step(u + 1, 0)
            read_ctx(LAST - 1)
            exponentials(LAST, masked[0], e_t[0])
            diagonals(LAST, SLOTS, False)
            read_ctx(LAST)
            relu(T, 0)
            exponentials(T, masked[1], e_t[1])
            diagonals(T, REST, False)
            read_ctx(T)
            dense_scalar(act)

        @block.vector
        def _(dve):
            def row_stats(t, b, loaded):
                alone(dve, loaded)
                nc.vector.bn_stats(stats[:, :], x_t[b][:, :]).then_inc(stats_step, 1)
                alone(dve, (stats_step, 3 * t + 1))
                nc.vector.bn_aggr(mean_var[:, :], stats[:, :]).then_inc(stats_step, 1)
                dve.wait_ge(stats_step, 3 * t + 2)
                nc.vector.tensor_scalar(neg_mean[:, :], mean_var[:, 0:1], -1.0, None, ALU.mult).then_inc(stats_step, 1)
                nc.vector.tensor_scalar(var_eps[:, :], mean_var[:, 1:2], EPS, None, ALU.add).then_inc(stats_made, 1)

            def scan(u, b, first=False):
                t = 2 * u + b
                n = SCAN * t
                alone(dve, (mask_in[b], 16 * u + 16))
                for g in range(J):
                    nc.vector.max(cand[:, g, :], mask[b][:, g * W:(g + 1) * W]).then_inc(scan_step, 1)
                alone(dve, (scan_step, n + J))
                for g in range(J):
                    ins = nc.vector.max_index(where[:, g, :], cand[:, g, :], mask[b][:, g * W:(g + 1) * W])
                    ins.then_inc(scan_step if g < J - 1 else mask_scanned, 1)
                n += 2 * J - 1
                dve.wait_ge(mask_scanned, t + 1)
                nc.vector.tensor_tensor(key_of[:, :, :], group_top[:, :, :], where[:, :, :], ALU.subtract).then_inc(scan_step, 1)
                nc.vector.tensor_tensor(is_expected[:, :, :], cand[:, :, :], expected[:, :, :], ALU.is_equal).then_inc(scan_step, 1)
                dve.wait_ge(scan_step, n + 1)
                nc.vector.scalar_tensor_tensor(edge_key[:, :, :], cand[:, :, :], 0.0, key_of[:, :, :],
                                               ALU.is_gt, ALU.mult).then_inc(scan_step, 1)
                dve.wait_ge(scan_step, n + 2)
                nc.vector.tensor_tensor(odd_all[:, bass.ds(t, 1), :].rearrange("p a n -> p (a n)"),
                                        is_expected[:, :, :].rearrange("p g n -> p (g n)"),
                                        cand[:, :, :].rearrange("p g n -> p (g n)"), ALU.not_equal).then_inc(scan_step, 1)
                alone(dve, (scan_step, n + 3))
                nc.vector.max(top_key[:, 0:TOP], edge_key[:, :, :]).then_inc(scan_step, 1)
                alone(dve, (scan_step, n + 5))
                nc.vector.match_replace(later_key[:, :, :], top_key[:, 0:TOP], edge_key[:, :, :], 0.0).then_inc(scan_step, 1)
                alone(dve, (scan_step, n + 6))
                nc.vector.max(top_key[:, TOP:REST], later_key[:, :, :]).then_inc(scan_step, 1)
                dve.wait_ge(scan_step, n + 7)
                if not first:
                    dve.wait_ge(recorded[b], 16 * u)
                nc.vector.tensor_scalar(record[b][:, 0:REST], top_key[:, :], -1.0, float(N), ALU.mult, ALU.add).then_inc(columns_made, 1)
                nc.vector.tensor_scalar(used[b][:, :], top_key[:, :], 0.0, None, ALU.is_gt).then_inc(used_made, 1)
                nc.vector.tensor_copy(record[b][:, REST:REST + 1], row_numbers[:, bass.ds(t, 1)]).then_inc(scan_step, 1)
                nc.vector.scalar_tensor_tensor(more_all[:, bass.ds(t, 1), :].rearrange("p a n -> p (a n)"),
                                               edge_key[:, :, :].rearrange("p g n -> p (g n)"), top_key[:, REST - 1:REST],
                                               edge_key[:, :, :].rearrange("p g n -> p (g n)"),
                                               ALU.is_lt, ALU.mult).then_inc(scan_step, 1)

            def find_place(t, b):
                dve.wait_ge(place_summed, t + 1)
                nc.vector.tensor_scalar(place_of[b][:, :], p_place[:, 0:1], float(FAR), None, ALU.add).then_inc(place_made, 1)
                nc.vector.tensor_tensor(flagged[:, :], flagged[:, :], used[b][:, SLOTS:SLOTS + 1], ALU.add).then_inc(flagged_made, 1)

            def read_q(t):
                dve.wait_ge(q_summed, t + 1)
                dve.wait_ge(rstd_made, t + 1)
                nc.vector.scalar_tensor_tensor(q_t[:, :], p_proj[:, :], rstd[:, :], b_scores[:, :],
                                               ALU.mult, ALU.add).then_inc(q_made, 1)
                nc.vector.scalar_tensor_tensor(shift[:, :], p_shift[:, 0:1], rstd[:, :], b_shift[:, :],
                                               ALU.mult, ALU.add).then_inc(q_made, 1)

            def edge_scores(t, loaded, edges_t, used_t, masked_t, slots):
                n = DOTS * t
                dve.wait_ge(*loaded)
                dve.wait_ge(q_made, 2 * t + 2)
                for s in range(slots):
                    if s >= 2:
                        dve.wait_ge(dot_step, n + s - 1)
                    nc.vector.tensor_tensor_reduce(out=product[s % 2], in0=edges_t[:, s, 0:D], in1=q_t[:, :],
                                                   scale=1.0, scalar=0.0, op0=ALU.mult, op1=ALU.add,
                                                   accum_out=dots[:, s:s + 1]).then_inc(dot_step, 1)
                n += slots
                dve.wait_ge(dot_step, n)
                nc.vector.tensor_scalar(scaled[:, 0:slots], dots[:, 0:slots], shift[:, :], INV, ALU.add, ALU.mult).then_inc(dot_step, 1)
                dve.wait_ge(dot_step, n + 1)
                nc.vector.tensor_tensor(scaled[:, 0:slots], scaled[:, 0:slots], used_t[:, 0:slots], ALU.mult).then_inc(dot_step, 1)
                dve.wait_ge(dot_step, n + 2)
                nc.vector.tensor_scalar(low[:, 0:slots], scaled[:, 0:slots], THRESHOLD, MASKED, ALU.is_lt, ALU.mult).then_inc(dot_step, 1)
                dve.wait_ge(dot_step, n + 3)
                nc.vector.scalar_tensor_tensor(low[:, 0:slots], scaled[:, 0:slots], -THRESHOLD, low[:, 0:slots],
                                               ALU.is_gt, ALU.mult).then_inc(dot_step, 1)
                dve.wait_ge(dot_step, n + 4)
                nc.vector.tensor_tensor(masked_t[:, 0:slots], scaled[:, 0:slots], low[:, 0:slots], ALU.add).then_inc(dot_step, 1)
                dve.wait_ge(dot_step, n + 5)
                nc.vector.reduce_max(row_max[:, :], masked_t[:, :], AX.X).then_inc(dot_step, 1)
                dve.wait_ge(dot_step, n + 6)
                nc.vector.tensor_scalar(neg_max[:, :], row_max[:, :], -1.0, None, ALU.mult).then_inc(max_made, 1)

            def edge_weights(t, e, slots):
                n = DOTS * t + slots + 6
                dve.wait_ge(exp_made, t + 1)
                nc.vector.tensor_scalar(weight[:, 0:slots], e[:, 0:slots], e[:, slots:slots + 1], 0.0,
                                        ALU.subtract, ALU.add, accum_out=weight_sum[:, :]).then_inc(weights_made, 1)
                dve.wait_ge(weights_made, t + 1)
                nc.vector.scalar_tensor_tensor(row_sum[:, :], e[:, slots:slots + 1], float(N), weight_sum[:, :],
                                               ALU.mult, ALU.add).then_inc(dot_step, 1)
                dve.wait_ge(dot_step, n + 1)
                nc.vector.reciprocal(inv_sum[:, :], row_sum[:, :]).then_inc(dot_step, 1)

            def read_ctx(t, e, slots):
                dve.wait_ge(ctx_summed, t + 1)
                nc.vector.scalar_tensor_tensor(ctx_t[:, :], value_sum, e[:, slots:slots + 1], p_ctx[:, :],
                                               ALU.mult, ALU.add).then_inc(ctx_made, 1)

            def finish(t, u, b, slots):
                dve.wait_ge(out_summed, t + 1)
                dve.wait_ge(x_bias_made, t + 1)
                dve.wait_ge(out_stored[b], 16 * u + 16)
                dve.wait_ge(dot_step, DOTS * t + slots + 8)
                nc.vector.scalar_tensor_tensor(out_t[b][:, :], p_out[:, :], inv_sum[:, :], x_bias[b][:, :],
                                               ALU.mult, ALU.add).then_inc(out_made, 1)

            dve.wait_ge(consts_made, 1)
            row_stats(0, 0, (x_in[0], 16))
            scan(0, 0, first=True)
            dve.wait_ge(products_read, C + 2)
            read_q(0)
            row_stats(1, 1, (x_in[1], 16))
            scan(0, 1, first=True)
            edge_scores(0, (edges_in[0], 16 * SLOTS), edges[0], used[0], masked[0], SLOTS)
            read_q(1)
            find_place(0, 0)
            find_place(1, 1)
            edge_weights(0, e_t[0], SLOTS)
            dve.wait_ge(products_read, PRODUCTS)

            def step(u, b):
                t = 2 * u + b
                un, bn = (u + 1, 0) if b else (u, 1)
                row_stats(t + 1, bn, (x_in[bn], 16 * un + 16))
                scan(un, bn)
                read_ctx(t - 1, e_t[0], SLOTS)
                edge_scores(t, (edges_in[b], 16 * SLOTS * u + 16 * SLOTS), edges[b], used[b], masked[0], SLOTS)
                read_q(t + 1)
                finish(t - 1, u if b else u - 1, bn, SLOTS)
                find_place(t + 1, bn)
                edge_weights(t, e_t[0], SLOTS)

            with dve.Fori(0, LAST // 2) as u:
                step(u, 1)
                step(u + 1, 0)
            u = T // 2
            read_ctx(LAST - 1, e_t[0], SLOTS)
            edge_scores(LAST, (edges_in[1], 16 * SLOTS * u), edges[1], used[1], masked[0], SLOTS)
            finish(LAST - 1, u - 1, 0, SLOTS)
            edge_weights(LAST, e_t[0], SLOTS)
            read_ctx(LAST, e_t[0], SLOTS)
            finish(LAST, u - 1, 1, SLOTS)
            row_stats(T, 0, (rest_in, 16))
            nc.vector.tensor_scalar(used[0][:, :], record[0][:, 0:REST], float(N), None, ALU.is_lt).then_inc(rest_used, 1)
            read_q(T)
            dve.wait_ge(rest_used, 1)
            edge_scores(T, (edges_in[0], 16 * SLOTS * u + 16 * REST), edges_kv, used[0], masked[1], REST)
            edge_weights(T, e_t[1], REST)
            read_ctx(T, e_t[1], REST)
            finish(T, u, 0, REST)
            nc.vector.reduce_sum(verdict[:, 0:1], odd_all, AX.XY).then_inc(verdict_step, 1)
            nc.vector.reduce_sum(verdict[:, 1:2], more_all, AX.XY).then_inc(verdict_step, 1)
            dve.wait_ge(mask_checked, T)
            nc.vector.reduce_sum(verdict[:, 2:3], negatives[:, :], AX.X).then_inc(verdict_step, 1)
            dve.wait_ge(verdict_step, 3)
            nc.vector.reduce_sum(verdict[:, 3:4], verdict[:, 0:3], AX.X).then_inc(verdict_step, 1)
            dve.wait_ge(verdict_step, 4)
            nc.vector.tensor_scalar(verdict[:, 4:5], verdict[:, 3:4], 0.0, None, ALU.is_equal).then_inc(verdict_step, 1)
            dve.wait_ge(verdict_summed, 1)
            nc.vector.tensor_scalar(verdict[:, 5:6], p_place[:, 1:2], float(P), None, ALU.is_equal).then_inc(verdict_step, 1)
            nc.vector.tensor_scalar(verdict[:, 6:7], p_place[:, 2:3], float(P), None, ALU.is_le).then_inc(verdict_step, 1)
            dve.wait_ge(verdict_step, 7)
            nc.vector.tensor_tensor(verdict_i[:, :], verdict[:, 5:6], verdict[:, 6:7], ALU.mult).then_inc(verdict_made, 1)
            dense_vector(dve)

        @block.tensor
        def _(pe):
            def project_q(t):
                pe.wait_ge(h_made, t + 1)
                for c in range(C):
                    last = nc.tensor.transpose(p_turn[:, c * P:(c + 1) * P], h_t[:, c * P:(c + 1) * P], ident[:, :])
                last.then_inc(h_turned, 1)
                pe.wait_ge(hT_made, t + 1)
                if not (isinstance(t, int) and t == 0):
                    pe.wait_ge(q_made, 2 * t)
                for c in range(C):
                    nc.tensor.matmul(p_proj[:, :], hT[:, c, :], w_scores[:, c, :], start=(c == 0), stop=(c == C - 1))
                for c in range(C):
                    last = nc.tensor.matmul(p_shift[:, 0:1], hT[:, c, :], w_shift[:, c:c + 1],
                                            start=(c == 0), stop=(c == C - 1))
                last.then_inc(q_summed, 1)

            def place(t, b, first=False):
                pe.wait_ge(used_made, t + 1)
                if not first:
                    pe.wait_ge(flagged_made, t)
                nc.tensor.matmul(p_place[:, 0:1], before[:, :], used[b][:, SLOTS:SLOTS + 1], start=True, stop=False)
                nc.tensor.matmul(p_place[:, 0:1], ones[:, :], flagged[:, :], start=False, stop=True).then_inc(place_summed, 1)

            def project_out(t):
                pe.wait_ge(ctx_made, t + 1)
                for c in range(C):
                    last = nc.tensor.transpose(p_turn_ctx[:, c * P:(c + 1) * P], ctx_t[:, c * P:(c + 1) * P], ident[:, :])
                last.then_inc(ctx_turned, 1)
                pe.wait_ge(ctxT_made, t + 1)
                for c in range(C):
                    last = nc.tensor.matmul(p_out[:, :], ctxT[:, c, :], w_out[:, c, :], start=(c == 0), stop=(c == C - 1))
                last.then_inc(out_summed, 1)

            def weigh(t, edges_t, slots):
                pe.wait_ge(diag_made, t + 1)
                for s in range(slots):
                    last = nc.tensor.matmul(p_ctx[:, :], diag[:, s, :], edges_t[:, s, D:2 * D],
                                            start=(s == 0), stop=(s == slots - 1))
                last.then_inc(ctx_summed, 1)

            def product_of(left, right, into):
                for c in range(C):
                    for k in range(C):
                        last = nc.tensor.matmul(p_weights[c][:, :], raw[left][:, k, c * P:(c + 1) * P],
                                                raw[right][:, k, :], start=(k == 0), stop=(k == C - 1))
                    last.then_inc(products, 1)

            pe.wait_ge(weights_in, 16 * 5)
            product_of("wq", "wk", w_scores)
            pe.wait_ge(wide_made, 2 * C)
            wide = [out_t[0], out_t[1]]
            for k in range(C):
                nc.tensor.matmul(p_ctx[:, :], wide[0][:, k * P:(k + 1) * P], raw["wk"][:, k, :],
                                 start=(k == 0), stop=(k == C - 1))
            for c in range(C):
                for k in range(C):
                    nc.tensor.matmul(p_shift[:, c:c + 1], raw["wq"][:, k, c * P:(c + 1) * P],
                                     bias_cols[:, 1, k:k + 1], start=(k == 0), stop=(k == C - 1))
            for k in range(C):
                last = nc.tensor.matmul(p_shift[:, C:C + 1], wide[0][:, k * P:(k + 1) * P], bias_cols[:, 1, k:k + 1],
                                        start=(k == 0), stop=(k == C - 1))
            last.then_inc(products, 1)
            pe.wait_ge(products_read, C + 2)
            project_q(0)
            pe.wait_ge(late_weights_in, 48)
            product_of("wv", "wmT", w_out)
            for k in range(C):
                last = nc.tensor.matmul(p_ctx[:, :], wide[1][:, k * P:(k + 1) * P], raw["wmT"][:, k, :],
                                        start=(k == 0), stop=(k == C - 1))
            last.then_inc(products, 1)
            pe.wait_ge(products_read, 2 * C + 3)
            for s in range(T // STAGED):
                pe.wait_ge(staged_in[s % 2], 16 * (s // 2) + 16)
                for i in range(STAGED):
                    last = nc.tensor.matmul(p_ctx[:, :], ones[:, :], staged[s % 2][:, i, :],
                                            start=(s == 0 and i == 0), stop=(s == T // STAGED - 1 and i == STAGED - 1))
                last.then_inc(staged_used if s < T // STAGED - 1 else products, 1)
            place(0, 0, first=True)
            project_q(1)
            place(1, 1)
            pe.wait_ge(products_read, PRODUCTS)
            weigh(0, edges[0], SLOTS)

            def step(t, b):
                project_q(t + 1)
                place(t + 1, 1 - b)
                project_out(t - 1)
                weigh(t, edges[b], SLOTS)

            with pe.Fori(1, LAST, 2) as t:
                step(t, 1)
                step(t + 1, 0)
            project_out(LAST - 1)
            weigh(LAST, edges[1], SLOTS)
            project_out(LAST)
            project_q(T)
            weigh(T, edges_kv, REST)
            project_out(T)
            pe.wait_ge(verdict_step, 5)
            nc.tensor.matmul(p_place[:, 1:2], ones[:, :], verdict[:, 4:5], start=True, stop=True)
            nc.tensor.matmul(p_place[:, 2:3], ones[:, :], flagged[:, :], start=True, stop=True).then_inc(verdict_summed, 1)
            dense_tensor(pe)


def kernel(**inputs):
    import numpy as np
    import concourse.bacc as bacc
    from concourse.bass_utils import run_bass_kernel_spmd

    def down(b):
        return np.ascontiguousarray(b.reshape(-1, P).T)

    g = {n.removeprefix("L0_gnn_"): np.asarray(a) for n, a in inputs.items()}
    laid = {
        "x": g["x"], "adj": g["adj"], "keyT": g["key"].T, "kv": np.concatenate([g["key"], g["value"]], axis=1),
        "wq": g["Wq"], "wk": g["Wk"], "wv": g["Wv"], "wmT": g["Wm"].T,
        "bq": down(g["bq"]), "bk": down(g["bk"]), "bv": down(g["bv"]), "bm": g["bm"],
    }
    nc = bacc.Bacc("TRN2", target_bir_lowering=False, num_devices=1)
    arrays, args = {}, {}
    for name, a in laid.items():
        a = np.ascontiguousarray(a)
        arrays[f"in_{name}"] = a
        args[name] = nc.dram_tensor(f"in_{name}", a.shape, mybir.dt.from_np(a.dtype), kind="ExternalInput").ap()
    args["records"] = nc.dram_tensor("records", (P, REST + 1), U32, kind="Internal").ap()
    args["out"] = nc.dram_tensor("out_0", g["x"].shape, F32, kind="ExternalOutput").ap()
    graph_attention(nc, **args)
    r = run_bass_kernel_spmd(nc, [arrays], core_ids=[0])
    return r.results[0]["out_0"]
```

```python
from contextlib import ExitStack

import concourse.bass as bass
from concourse import mybir

F32 = mybir.dt.float32
BF16 = mybir.dt.bfloat16
U32 = mybir.dt.uint32
I32 = mybir.dt.int32
ALU = mybir.AluOpType
ACT = mybir.ActivationFunctionType
AX = mybir.AxisListType
P = 128
MASKED = -1e9
THRESHOLD = 1e-5
EPS = 1e-5
TOP = 8
SLOTS = TOP
REST = 2 * TOP
FAR = 1000
GROUPS = 4


def graph_attention(nc, x, adj, keyT, valueT, kv, wq, wk, wv, wmT, bq, bk, bv, bm, records, out):
    N, D = x.shape
    T = N // P
    C = D // P
    W = 512
    J = N // W
    G = W // P
    INV = 1.0 / float(N) ** 0.5
    GW = N // GROUPS
    PARTS = 2
    SCAN = 2 * GROUPS + 8
    DOTS = SLOTS + 9
    HALF = SLOTS // 2
    assert N % (2 * P) == 0 and D == W and T > 6 and C * PARTS == 8

    with ExitStack() as ctx:
        def sb(name, shape, dt=F32):
            return ctx.enter_context(nc.sbuf_tensor(name, shape, dt))

        def sem(name):
            return ctx.enter_context(nc.semaphore(name))

        w_scores = sb("w_scores", [P, C, D])
        w_out = sb("w_out", [P, C, D])
        w_shift = sb("w_shift", [P, C])
        b_scores = sb("b_scores", [P, D])
        b_out = sb("b_out", [P, D])
        b_shift = sb("b_shift", [P, 1])
        ident = sb("ident", [P, P])
        ones = sb("ones", [P, P])
        bias_cols = sb("bias_cols", [P, 3, C])
        half = sb("half", [P, 1])

        keys_T = sb("keys_T", [P, C, N])
        values = sb("values", [P, T, D])
        scores = sb("scores", [P, N])
        adj_t = sb("adj_t", [P, N])

        edges_kv = keys_T[:, :, :].rearrange("p c n -> p (c n)").rearrange("p (s n) -> p s n", n=2 * D)
        edges = [edges_kv[:, b * SLOTS:(b + 1) * SLOTS, :] for b in range(2)]
        values_flat = values[:, :, :].rearrange("p t n -> p (t n)")
        mask = [values_flat[:, b * N:(b + 1) * N] for b in range(2)]
        rest_edges = [edges[0], values_flat[:, 0:2 * N].rearrange("p (s n) -> p s n", n=2 * D)]
        raw_flat = values_flat[:, 2 * N:4 * N]
        raw = {n: raw_flat[:, i * C * D:(i + 1) * C * D].rearrange("p (k n) -> p k n", k=C)
               for i, n in enumerate(("wq", "wk", "wv", "wmT"))}
        second_edges = keys_T[:, 2:4, :].rearrange("p c (k n) -> p (c k) n", k=PARTS)
        part = [second_edges[:, i, :] for i in range(4)]
        part += [raw_flat[:, i % 2 * N // PARTS:(i % 2 + 1) * N // PARTS] for i in range(4, C * PARTS)]
        flags = T * GROUPS * TOP
        flags_bf16 = scores[:, 0:flags].bitcast(BF16).rearrange("p (k t n) -> p k t n", k=2, t=T)
        odd_all = flags_bf16[:, 0]
        more_all = flags_bf16[:, 1]
        product = [scores[:, flags + b * D:flags + (b + 1) * D] for b in range(2)]
        value_sum = scores[:, flags + 2 * D:flags + 3 * D]
        junk = adj_t[:, 0:N // 2].bitcast(BF16)
        diag = adj_t[:, N // 2:N // 2 + SLOTS * P].rearrange("p (s n) -> p s n", s=SLOTS)
        spread = adj_t[:, N // 2 + SLOTS * P:].rearrange("p (s n) -> p s n", s=C * PARTS)
        bm_wide = scores[:, flags + 3 * D:flags + 4 * D]
        square_junk = scores[:, flags + 4 * D:flags + 4 * D + D // 2].bitcast(BF16)

        x_t = [sb(f"x_t{b}", [P, D]) for b in range(2)]
        x_bias = [sb(f"x_bias{b}", [P, D]) for b in range(2)]
        out_t = [sb(f"out_t{b}", [P, D]) for b in range(2)]
        row_total = sb("row_total", [P, 1])
        var_total = sb("var_total", [P, 1])
        stats = sb("stats", [P, 6])
        mean_var = sb("mean_var", [P, 2])
        var_eps = sb("var_eps", [P, 1])
        rstd = sb("rstd", [P, 1])
        neg_mean = sb("neg_mean", [P, 1])
        h_t = sb("h_t", [P, D])
        hT = sb("hT", [P, C, P])
        q_t = sb("q_t", [P, D])
        shift = sb("shift", [P, 1])
        ctx_t = sb("ctx_t", [P, D])
        ctxT = sb("ctxT", [P, C, P])

        cand = sb("cand", [P, GROUPS, TOP])
        where = sb("where", [P, GROUPS, TOP], U32)
        group_top = sb("group_top", [P, GROUPS, TOP])
        expected = sb("expected", [P, GROUPS, TOP])
        is_expected = sb("is_expected", [P, GROUPS, TOP])
        key_of = sb("key_of", [P, GROUPS, TOP])
        edge_key = sb("edge_key", [P, GROUPS, TOP])
        later_key = sb("later_key", [P, GROUPS, TOP])
        top_key = sb("top_key", [P, REST])
        record = [sb(f"record{b}", [P, REST + 1], U32) for b in range(2)]
        used = [sb(f"used{b}", [P, REST]) for b in range(2)]
        row_numbers = sb("row_numbers", [P, T], U32)
        place_of = [sb(f"place_of{b}", [P, 1], U32) for b in range(2)]
        before = sb("before", [P, P])
        flagged = sb("flagged", [P, 1])
        blank = sb("blank", [P, REST + 1], U32)
        negatives = sb("negatives", [P, T])
        dots = sb("dots", [P, REST])
        scaled = sb("scaled", [P, REST])
        low = sb("low", [P, REST])
        masked = [sb("masked", [P, SLOTS + 1]), sb("masked_rest", [P, REST + 1])]
        row_max = sb("row_max", [P, 1])
        neg_max = sb("neg_max", [P, 1])
        e_t = [sb("e_t", [P, SLOTS + 1]), sb("e_rest", [P, REST + 1])]
        above_w0 = sb("above_w0", [P, REST])
        weight = sb("weight", [P, REST])
        w0 = sb("w0", [P, 1])
        diag_w0 = sb("diag_w0", [P, P])
        part_sums = sb("part_sums", [P, C, PARTS])
        weight_sum = sb("weight_sum", [P, 1])
        row_sum = sb("row_sum", [P, 1])
        inv_sum = sb("inv_sum", [P, 1])
        verdict = sb("verdict", [P, 8])
        verdict_i = sb("verdict_i", [P, 1], I32)

        bank = [ctx.enter_context(nc.psum_tensor(f"bank{i}", [P, W], F32)) for i in range(8)]
        p_turn, p_proj, p_shift, p_place, p_ctx, p_out, p_turn_ctx, p_spare = bank
        p_scores_weights = [p_place, p_out, p_turn_ctx, p_spare]
        p_out_weights = [p_out, p_turn_ctx, p_spare, p_ctx]

        weights_in = sem("weights_in")
        late_weights_in = sem("late_weights_in")
        zeros_made = sem("zeros_made")
        consts_made = sem("consts_made")
        wide_made = sem("wide_made")
        products = sem("products")
        products_read = sem("products_read")
        bias_done = sem("bias_done")
        part_in = [sem(f"part_in{i}") for i in range(C * PARTS)]
        parts_summed = sem("parts_summed")
        parts_spread = sem("parts_spread")
        x_kept = sem("x_kept")
        blank_in = sem("blank_in")
        x_in = [sem(f"x_in{b}") for b in range(2)]
        mask_in = [sem(f"mask_in{b}") for b in range(2)]
        stats_step = sem("stats_step")
        stats_made = sem("stats_made")
        var_made = sem("var_made")
        rstd_made = sem("rstd_made")
        h_made = sem("h_made")
        h_turned = sem("h_turned")
        hT_made = sem("hT_made")
        q_summed = sem("q_summed")
        shift_summed = sem("shift_summed")
        q_made = sem("q_made")
        scan_step = sem("scan_step")
        mask_scanned = sem("mask_scanned")
        mask_checked = sem("mask_checked")
        columns_made = sem("columns_made")
        used_made = sem("used_made")
        place_summed = sem("place_summed")
        place_made = sem("place_made")
        flagged_made = sem("flagged_made")
        recorded = [sem(f"recorded{b}") for b in range(2)]
        edges_in = [[sem(f"edges_in{b}_{h}") for h in range(2)] for b in range(2)]
        dot_step = sem("dot_step")
        max_made = sem("max_made")
        exp_made = sem("exp_made")
        weights_made = sem("weights_made")
        diag_made = sem("diag_made")
        diag_w0_made = sem("diag_w0_made")
        edges_used = sem("edges_used")
        ctx_summed = sem("ctx_summed")
        ctx_made = sem("ctx_made")
        ctx_turned = sem("ctx_turned")
        ctxT_made = sem("ctxT_made")
        out_summed = sem("out_summed")
        out_read = sem("out_read")
        x_bias_made = sem("x_bias_made")
        out_made = sem("out_made")
        out_stored = [sem(f"out_stored{b}") for b in range(2)]
        rest_listed = sem("rest_listed")
        rest_in = sem("rest_in")
        rest_edges_in = [sem(f"rest_edges_in{h}") for h in range(REST // HALF)]
        rest_used = sem("rest_used")
        rest_step = sem("rest_step")
        rest_made = sem("rest_made")
        rest_stored = sem("rest_stored")
        verdict_step = sem("verdict_step")
        verdict_summed = sem("verdict_summed")
        verdict_made = sem("verdict_made")

        below = out_t[1]
        d_probs_T = x_t[1], x_bias[1]
        d_names = ("keys_in values_in x_in adj_in x_used adj_used stats_step stats_made rstd_made h_made turned "
                   "turn_read q_summed q_made scores_summed scores_read mask_step max_made exp_made probs_turned "
                   "probs_read ctx_summed ctx_made out_summed out_made out_stored").split()
        d = {name: sem(f"d_{name}") for name in d_names}
        p_scores, p_probs = (p_place, p_out), (p_turn_ctx, p_spare)

        def if_dense(eng):
            eng.wait_ge(verdict_made, 1)
            return eng.If(eng.value_load(verdict_i[0:1, 0:1], min_val=0, max_val=1) < 1)

        def dense_sync(sp):
            with if_dense(sp):
                sp.dma_start(keys_T[:, :, :], keyT.rearrange("(k p) n -> p k n", p=P)).then_inc(d["keys_in"], 16)
                sp.dma_start(values[:, :, :], kv[:, D:2 * D].rearrange("(t p) n -> p t n", p=P)).then_inc(d["values_in"], 16)
                sp.sem_inc(d["out_stored"], 16)
                with sp.Fori(0, T) as t:
                    row = sp.snap(t * P)
                    sp.wait_ge(d["x_used"], t + 1)
                    sp.dma_start(x_t[0][:, :], x[bass.ds(row, P), :]).then_inc(d["x_in"], 16)
                    sp.wait_ge(d["adj_used"], t + 1)
                    sp.dma_start(adj_t[:, :], adj[bass.ds(row, P), :]).then_inc(d["adj_in"], 16)
                    sp.wait_ge(d["out_made"], t + 1)
                    sp.dma_start(out[bass.ds(row, P), :], out_t[0][:, :]).then_inc(d["out_stored"], 16)
                sp.wait_ge(d["out_stored"], 16 * T + 16)

        def dense_gpsimd(pool):
            with if_dense(pool), pool.Fori(0, T) as t:
                pool.wait_ge(d["stats_made"], t + 1)
                nc.gpsimd.tensor_tensor(rstd[:, :], var_eps[:, :], half[:, :], ALU.pow).then_inc(d["rstd_made"], 1)

        def dense_scalar(act):
            def read_turned(to, n):
                act.wait_ge(d["turned"], n)
                nc.scalar.copy(to[:, :, :], p_turn[:, :].rearrange("p (c n) -> p c n", c=C)).then_inc(d["turn_read"], 1)

            with if_dense(act), act.Fori(0, T) as t:
                act.wait_ge(d["stats_made"], t + 1)
                nc.scalar.activation(h_t[:, :], x_t[0][:, :], ACT.Relu, bias=neg_mean[:, :]).then_inc(d["h_made"], 1)
                read_turned(hT, 3 * t + 1)
                read_turned(ctxT, 3 * t + 2)
                for j in range(J):
                    act.wait_ge(d["scores_summed"], J * t + j + 1)
                    nc.scalar.activation(scores[:, j * W:(j + 1) * W], p_scores[j % 2][:, :], ACT.Identity,
                                         bias=shift[:, :], scale=INV).then_inc(d["scores_read"], 1)
                act.wait_ge(d["max_made"], t + 1)
                nc.scalar.activation(scores[:, :], scores[:, :], ACT.Exp, bias=neg_max[:, :],
                                     accum_out=row_sum[:, :]).then_inc(d["exp_made"], 1)
                read_turned(ctxT, 3 * t + 3)

        def dense_vector(dve):
            STATS, MASKS = 3, 4 * J + 1
            with if_dense(dve):
                dve.sem_inc(d["x_used"], 1)
                dve.sem_inc(d["adj_used"], 1)
                with dve.Fori(0, T) as t:
                    alone(dve, (d["x_in"], 16 * t + 16))
                    nc.vector.bn_stats(stats[:, :], x_t[0][:, :]).then_inc(d["stats_step"], 1)
                    alone(dve, (d["stats_step"], STATS * t + 1))
                    nc.vector.bn_aggr(mean_var[:, :], stats[:, :]).then_inc(d["stats_step"], 1)
                    dve.wait_ge(d["stats_step"], STATS * t + 2)
                    nc.vector.tensor_scalar(neg_mean[:, :], mean_var[:, 0:1], -1.0, None, ALU.mult).then_inc(d["stats_step"], 1)
                    nc.vector.tensor_scalar(var_eps[:, :], mean_var[:, 1:2], EPS, None, ALU.add).then_inc(d["stats_made"], 1)
                    dve.wait_ge(d["q_summed"], t + 1)
                    dve.wait_ge(d["rstd_made"], t + 1)
                    nc.vector.scalar_tensor_tensor(q_t[:, :], p_proj[:, :], rstd[:, :], b_scores[:, :],
                                                   ALU.mult, ALU.add).then_inc(d["q_made"], 1)
                    nc.vector.scalar_tensor_tensor(shift[:, :], p_shift[:, 0:1], rstd[:, :], b_shift[:, :],
                                                   ALU.mult, ALU.add).then_inc(d["q_made"], 1)
                    dve.wait_ge(d["adj_in"], 16 * t + 16)
                    for j in range(J):
                        own = scores[:, j * W:(j + 1) * W]
                        n = MASKS * t + 4 * j
                        dve.wait_ge(d["scores_read"], J * t + j + 1)
                        nc.vector.tensor_tensor(own, own, adj_t[:, j * W:(j + 1) * W], ALU.mult).then_inc(d["mask_step"], 1)
                        dve.wait_ge(d["mask_step"], n + 1)
                        nc.vector.tensor_scalar(below[:, :], own, THRESHOLD, MASKED, ALU.is_lt, ALU.mult).then_inc(d["mask_step"], 1)
                        dve.wait_ge(d["mask_step"], n + 2)
                        nc.vector.scalar_tensor_tensor(below[:, :], own, -THRESHOLD, below[:, :],
                                                       ALU.is_gt, ALU.mult).then_inc(d["mask_step"], 1)
                        dve.wait_ge(d["mask_step"], n + 3)
                        nc.vector.tensor_tensor(own, own, below[:, :], ALU.add).then_inc(d["mask_step"], 1)
                    dve.wait_ge(d["mask_step"], MASKS * t + 4 * J)
                    nc.vector.tensor_scalar(mean_var[:, 0:1], shift[:, :], 1.0, None, ALU.mult).then_inc(d["adj_used"], 1)
                    nc.vector.reduce_max(row_max[:, :], scores[:, :], AX.X).then_inc(d["mask_step"], 1)
                    dve.wait_ge(d["mask_step"], MASKS * t + MASKS)
                    nc.vector.tensor_scalar(neg_max[:, :], row_max[:, :], -1.0, None, ALU.mult).then_inc(d["max_made"], 1)
                    for j in range(J):
                        dve.wait_ge(d["probs_turned"], J * t + j + 1)
                        nc.vector.tensor_copy(d_probs_T[j % 2][:, :], p_probs[j % 2][:, :]).then_inc(d["probs_read"], 1)
                    dve.wait_ge(d["exp_made"], t + 1)
                    nc.vector.reciprocal(inv_sum[:, :], row_sum[:, :]).then_inc(d["ctx_made"], 1)
                    dve.wait_ge(d["ctx_made"], 2 * t + 1)
                    dve.wait_ge(d["ctx_summed"], t + 1)
                    nc.vector.tensor_scalar(ctx_t[:, :], p_ctx[:, :], inv_sum[:, :], None, ALU.mult).then_inc(d["ctx_made"], 1)
                    nc.vector.tensor_tensor(x_bias[0][:, :], x_t[0][:, :], b_out[:, :], ALU.add).then_inc(d["x_used"], 1)
                    dve.wait_ge(d["x_used"], t + 2)
                    dve.wait_ge(d["out_summed"], t + 1)
                    dve.wait_ge(d["out_stored"], 16 * t + 16)
                    nc.vector.tensor_tensor(out_t[0][:, :], p_proj[:, :], x_bias[0][:, :], ALU.add).then_inc(d["out_made"], 1)

        def dense_tensor(pe):
            def turn(source, into, count):
                for c in range(C):
                    last = nc.tensor.transpose(into[:, c * P:(c + 1) * P], source[:, c * P:(c + 1) * P], ident[:, :])
                last.then_inc(count, 1)

            with if_dense(pe):
                pe.wait_ge(d["keys_in"], 16)
                pe.wait_ge(d["values_in"], 16)
                with pe.Fori(0, T) as t:
                    pe.wait_ge(d["h_made"], t + 1)
                    turn(h_t, p_turn, d["turned"])
                    pe.wait_ge(d["turn_read"], 3 * t + 1)
                    for c in range(C):
                        nc.tensor.matmul(p_proj[:, :], hT[:, c, :], w_scores[:, c, :], start=(c == 0), stop=(c == C - 1))
                    for c in range(C):
                        last = nc.tensor.matmul(p_shift[:, 0:1], hT[:, c, :], w_shift[:, c:c + 1],
                                                start=(c == 0), stop=(c == C - 1))
                    last.then_inc(d["q_summed"], 1)
                    pe.wait_ge(d["q_made"], 2 * t + 2)
                    turn(q_t, p_turn, d["turned"])
                    pe.wait_ge(d["turn_read"], 3 * t + 2)
                    for j in range(J):
                        if j >= 2:
                            pe.wait_ge(d["scores_read"], J * t + j - 1)
                        for c in range(C):
                            last = nc.tensor.matmul(p_scores[j % 2][:, :], ctxT[:, c, :], keys_T[:, c, j * W:(j + 1) * W],
                                                    start=(c == 0), stop=(c == C - 1))
                        last.then_inc(d["scores_summed"], 1)
                    pe.wait_ge(d["exp_made"], t + 1)
                    turn(scores[:, 0:W], p_probs[0], d["probs_turned"])
                    for j in range(J):
                        if j + 1 < J:
                            if j >= 1:
                                pe.wait_ge(d["probs_read"], J * t + j)
                            turn(scores[:, (j + 1) * W:(j + 2) * W], p_probs[(j + 1) % 2], d["probs_turned"])
                        pe.wait_ge(d["probs_read"], J * t + j + 1)
                        for g in range(G):
                            last = nc.tensor.matmul(p_ctx[:, :], d_probs_T[j % 2][:, g * P:(g + 1) * P],
                                                    values[:, j * G + g, :],
                                                    start=(j == 0 and g == 0), stop=(j == J - 1 and g == G - 1))
                    last.then_inc(d["ctx_summed"], 1)
                    pe.wait_ge(d["ctx_made"], 2 * t + 2)
                    turn(ctx_t, p_turn, d["turned"])
                    pe.wait_ge(d["turn_read"], 3 * t + 3)
                    for c in range(C):
                        last = nc.tensor.matmul(p_proj[:, :], ctxT[:, c, :], w_out[:, c, :], start=(c == 0), stop=(c == C - 1))
                    last.then_inc(d["out_summed"], 1)

        block = ctx.enter_context(nc.Block())
        LAST = T - 1
        PRODUCTS = 2 * C + 4

        def alone(eng, *waits):
            waits = [(semaphore, value if isinstance(value, int) else eng.to_reg(value)) for semaphore, value in waits]
            eng.wait_ge(consts_made, 1)
            for semaphore, value in waits:
                eng.wait_ge(semaphore, value)

        @block.sync
        def _(sp):
            def load_x(t, b):
                sp.dma_start(x_t[b][:, :], x[bass.ts(t, P), :]).then_inc(x_in[b], 16)

            def load_mask(t, b):
                sp.dma_start(mask[b], adj[bass.ts(t, P), :]).then_inc(mask_in[b], 16)

            for name, src in (("wq", wq), ("wk", wk)):
                sp.dma_start(raw[name], src.rearrange("(k p) n -> p k n", p=P)).then_inc(weights_in, 16)
            for i, src in enumerate((bq, bk, bv)):
                sp.dma_start(bias_cols[:, i, :], src).then_inc(weights_in, 16)
            for t in range(2):
                load_x(t, t)
                load_mask(t, t)
            for name, src in (("wv", wv), ("wmT", wmT)):
                sp.dma_start(raw[name], src.rearrange("(k p) n -> p k n", p=P)).then_inc(late_weights_in, 16)
            sp.dma_start(bm_wide, bm.partition_broadcast(P)).then_inc(late_weights_in, 16)

            def load_part(i):
                src = valueT[i // PARTS * P:(i // PARTS + 1) * P, i % PARTS * (N // PARTS):(i % PARTS + 1) * (N // PARTS)]
                sp.dma_start(part[i], src).then_inc(part_in[i], 16)

            for i in range(4):
                load_part(i)
            sp.wait_ge(consts_made, 1)
            sp.dma_start(records, blank[:, :]).then_inc(blank_in, 16)
            for b in range(2):
                sp.sem_inc(out_stored[b], 16)

            def next_mask(t, b):
                sp.wait_ge(mask_scanned, t - 1)
                sp.wait_ge(mask_checked, t - 1)
                load_mask(t, b)

            def next_x(t, b):
                sp.wait_ge(x_bias_made, t - 1)
                sp.wait_ge(stats_made, t - 1)
                load_x(t, b)

            def store(t, b):
                sp.wait_ge(out_made, t + 1)
                sp.dma_start(out[bass.ts(t, P), :], out_t[b][:, :]).then_inc(out_stored[b], 16)

            next_mask(2, 0)
            sp.wait_ge(x_kept, 1)
            sp.wait_ge(stats_made, 1)
            load_x(2, 0)
            sp.wait_ge(products, C + 1)
            for i in range(4, C * PARTS):
                if i >= 6:
                    sp.wait_ge(parts_summed, i - 1)
                load_part(i)
            next_mask(3, 1)
            sp.wait_ge(x_kept, 2)
            sp.wait_ge(stats_made, 2)
            load_x(3, 1)
            next_mask(4, 0)
            with sp.Fori(1, T // 2 - 2) as u:
                for b in range(2):
                    store(2 * u + b - 2, b)
                    next_x(2 * u + b + 2, b)
                    next_mask(2 * u + b + 3, 1 - b)
            store(T - 6, 0)
            next_x(T - 2, 0)
            next_mask(T - 1, 1)
            store(T - 5, 1)
            next_x(T - 1, 1)
            store(T - 4, 0)
            for b in range(2):
                sp.wait_ge(recorded[b], 16 * (T // 2))
            sp.dma_start(record[0][:, :], records).then_inc(rest_listed, 16)
            store(T - 3, 1)
            store(T - 2, 0)
            store(T - 1, 1)
            for b in range(2):
                sp.wait_ge(out_stored[b], 16 * (T // 2) + 16)
            sp.wait_ge(rest_stored, 16)
            dense_sync(sp)

        @block.gpsimd
        def _(pool):
            for tile, value in ((ident, 0.0), (ones, 1.0), (before, 1.0), (half, -0.5), (expected, 1.0),
                                (flagged, 0.0), (masked[0], MASKED), (masked[1], MASKED)):
                nc.gpsimd.memset(tile[:], value).then_inc(zeros_made, 1)
            for g in range(GROUPS):
                nc.gpsimd.memset(group_top[:, g, :], float(N - g * GW)).then_inc(zeros_made, 1)
            nc.gpsimd.iota(row_numbers[:, :], pattern=[[P, T]], base=0, channel_multiplier=1).then_inc(zeros_made, 1)
            nc.gpsimd.iota(blank[:, :], pattern=[[0, REST + 1]], base=N, channel_multiplier=0).then_inc(zeros_made, 1)
            made = 8 + GROUPS + 2
            pool.wait_ge(zeros_made, made)
            nc.gpsimd.memset(expected[:, :, TOP - 1:TOP], 2.0).then_inc(zeros_made, 1)
            nc.gpsimd.affine_select(out=ident[:, :], in_=ident[:, :], compare_op=ALU.not_equal, fill=1.0,
                                    base=0, pattern=[[-1, P]], channel_multiplier=1).then_inc(zeros_made, 1)
            nc.gpsimd.affine_select(out=before[:, :], in_=before[:, :], compare_op=ALU.is_gt, fill=0.0,
                                    base=0, pattern=[[1, P]], channel_multiplier=-1).then_inc(zeros_made, 1)
            pool.wait_ge(zeros_made, made + 3)
            nc.gpsimd.affine_select(out=before[:, :], in_=before[:, :], compare_op=ALU.not_equal, fill=-float(FAR),
                                    base=0, pattern=[[1, P]], channel_multiplier=-1).then_inc(zeros_made, 1)
            pool.wait_ge(zeros_made, made + 4)
            nc.gpsimd.memset(half[:, :], -0.5).then_inc(consts_made, 1)
            nc.gpsimd.memset(edges[0], 0.0).then_inc(zeros_made, 1)

            def make_rstd(t):
                if isinstance(t, int) and t == 0:
                    pool.wait_ge(stats_made, 1)
                else:
                    alone(pool, (stats_made, t + 1), (q_made, 2 * t))
                nc.gpsimd.tensor_scalar(var_eps[:, :], var_total[:, :], 1.0 / D, EPS, ALU.mult, ALU.add).then_inc(var_made, 1)
                pool.wait_ge(var_made, t + 1)
                nc.gpsimd.tensor_tensor(rstd[:, :], var_eps[:, :], half[:, :], ALU.pow).then_inc(rstd_made, 1)

            def gather_slot(into, column, arrived):
                nc.gpsimd.indirect_dma_start(
                    out=into, out_offset=None, in_=kv, in_offset=bass.IndirectOffsetOnAxis(ap=column, axis=0),
                    bounds_check=N - 1, oob_is_err=False).then_inc(arrived, 16)

            def gather_half(b, h):
                for s in range(h * HALF, (h + 1) * HALF):
                    gather_slot(edges[b][:, s, :], record[b][:, s:s + 1], edges_in[b][h])

            def gather(t, b, *free):
                alone(pool, (columns_made, t + 1), *free)
                for h in range(2):
                    gather_half(b, h)

            def add_bias(t, b):
                if not (isinstance(t, int) and t < 2):
                    pool.wait_ge(out_made, t - 1)
                nc.gpsimd.tensor_tensor(x_bias[b][:, :], x_t[b][:, :], b_out[:, :], ALU.add).then_inc(x_bias_made, 1)

            def finish(t, b):
                pool.wait_ge(out_read, t + 1)
                pool.wait_ge(x_bias_made, t + 1)
                nc.gpsimd.tensor_tensor(out_t[b][:, :], out_t[b][:, :], x_bias[b][:, :], ALU.add).then_inc(out_made, 1)

            def note(t, b):
                alone(pool, (place_made, t + 1))
                nc.gpsimd.indirect_dma_start(
                    out=records, out_offset=bass.IndirectOffsetOnAxis(ap=place_of[b][:, :], axis=0),
                    in_=record[b][:, :], in_offset=None,
                    bounds_check=P - 1, oob_is_err=False).then_inc(recorded[b], 16)

            def keep_x(t):
                pool.wait_ge(h_made, t + 1)
                nc.gpsimd.tensor_copy(x_bias[t][:, :], x_t[t][:, :]).then_inc(x_kept, 1)

            make_rstd(0)
            keep_x(0)
            pool.wait_ge(zeros_made, made + 5)
            gather(0, 0)
            pool.wait_ge(blank_in, 16)
            note(0, 0)
            make_rstd(1)
            keep_x(1)
            pool.wait_ge(parts_summed, 4)
            gather(1, 1)
            note(1, 1)
            pool.wait_ge(late_weights_in, 48)
            pool.wait_ge(products_read, 2 * C + 3)
            nc.gpsimd.tensor_tensor(b_out[:, :], b_out[:, :], bm_wide, ALU.add).then_inc(bias_done, 1)
            pool.wait_ge(bias_done, 1)
            pool.wait_ge(x_kept, 2)
            for t in range(2):
                nc.gpsimd.tensor_tensor(x_bias[t][:, :], x_bias[t][:, :], b_out[:, :], ALU.add).then_inc(x_bias_made, 1)
            make_rstd(2)
            gather(2, 0, (edges_used, 1))
            note(2, 0)

            def step(u, b):
                t = 2 * u + b
                finish(t - 2, b)
                add_bias(t, b)
                make_rstd(t + 1)
                gather(t + 1, 1 - b, (edges_used, t))
                note(t + 1, 1 - b)

            with pool.Fori(1, T // 2 - 1) as u:
                step(u, 0)
                step(u, 1)
            finish(LAST - 3, 0)
            add_bias(LAST - 1, 0)
            make_rstd(LAST)
            alone(pool, (columns_made, T), (edges_used, LAST - 1))
            gather_half(1, 0)
            note(LAST, 1)
            alone(pool)
            gather_half(1, 1)
            finish(LAST - 2, 1)
            add_bias(LAST, 1)
            pool.wait_ge(rest_listed, 16)
            pool.wait_ge(stats_made, LAST)
            nc.gpsimd.indirect_dma_start(
                out=x_t[0][:, :], out_offset=None, in_=x,
                in_offset=bass.IndirectOffsetOnAxis(ap=record[0][:, REST:REST + 1], axis=0),
                bounds_check=N - 1, oob_is_err=False).then_inc(rest_in, 16)
            pool.wait_ge(mask_scanned, T)
            pool.wait_ge(mask_checked, T)
            for s in range(SLOTS, REST):
                gather_slot(rest_edges[1][:, s - SLOTS, :], record[0][:, s:s + 1], rest_edges_in[s // HALF])
            make_rstd(T)
            pool.wait_ge(edges_used, LAST)
            for s in range(SLOTS):
                gather_slot(rest_edges[0][:, s, :], record[0][:, s:s + 1], rest_edges_in[s // HALF])
            finish(LAST - 1, 0)
            pool.wait_ge(rest_in, 16)
            add_bias(T, 0)
            finish(LAST, 1)
            pool.wait_ge(rest_made, 1)
            for b in range(2):
                pool.wait_ge(out_stored[b], 16 * (T // 2) + 16)
            nc.gpsimd.indirect_dma_start(
                out=out, out_offset=bass.IndirectOffsetOnAxis(ap=record[0][:, REST:REST + 1], axis=0),
                in_=out_t[0][:, :], in_offset=None,
                bounds_check=N - 1, oob_is_err=False).then_inc(rest_stored, 16)
            pool.wait_ge(rest_stored, 16)
            dense_gpsimd(pool)

        @block.scalar
        def _(act):
            def make_h(t, b, *loaded):
                act.wait_ge(*loaded)
                nc.scalar.activation(h_t[:, :], x_t[b][:, :], ACT.Identity, accum_out=row_total[:, :]).then_inc(stats_step, 1)
                act.wait_ge(stats_step, 2 * t + 1)
                nc.scalar.activation(neg_mean[:, :], row_total[:, :], ACT.Copy, scale=-1.0 / D).then_inc(stats_step, 1)
                act.wait_ge(stats_step, 2 * t + 2)
                nc.scalar.activation(h_t[:, :], x_t[b][:, :], ACT.Relu, bias=neg_mean[:, :]).then_inc(h_made, 1)
                if not (isinstance(t, int) and t == 0):
                    act.wait_ge(rstd_made, t)
                nc.scalar.activation(square_junk[:, :], x_t[b][:, :], ACT.Square, bias=neg_mean[:, :],
                                     accum_out=var_total[:, :]).then_inc(stats_made, 1)

            def turn_h(t):
                act.wait_ge(h_turned, t + 1)
                nc.scalar.copy(hT[:, :, :], p_turn[:, :].rearrange("p (c n) -> p c n", c=C)).then_inc(hT_made, 1)

            def check_mask(u, b):
                act.wait_ge(mask_in[b], 16 * u + 16)
                nc.scalar.activation(junk, mask[b], ACT.Relu, scale=-1.0,
                                     accum_out=negatives[:, bass.ds(2 * u + b, 1)]).then_inc(mask_checked, 1)

            def read_ctx(t):
                act.wait_ge(ctx_summed, t + 1)
                nc.scalar.copy(ctx_t[:, :], p_ctx[:, :]).then_inc(ctx_made, 1)

            def turn_ctx(t):
                act.wait_ge(ctx_turned, t + 1)
                nc.scalar.copy(ctxT[:, :, :], p_turn_ctx[:, :].rearrange("p (c n) -> p c n", c=C)).then_inc(ctxT_made, 1)

            def exponentials(t, masked_t, e):
                act.wait_ge(max_made, t + 1)
                nc.scalar.activation(e[:, :], masked_t[:, :], ACT.Exp, bias=neg_max[:, :]).then_inc(exp_made, 1)

            def diagonals(t, slots):
                act.wait_ge(weights_made, t + 1)
                if not (isinstance(t, int) and t == 0):
                    act.wait_ge(ctx_summed, t)
                for s in range(slots):
                    ins = nc.scalar.activation(diag[:, s, :], ident[:, :], ACT.Copy, scale=weight[:, s:s + 1])
                    if (s + 1) % HALF == 0:
                        ins.then_inc(diag_made, 1)
                nc.scalar.activation(diag_w0[:, :], ident[:, :], ACT.Copy, scale=w0[:, :]).then_inc(diag_w0_made, 1)

            def sum_part(i):
                act.wait_ge(part_in[i], 16)
                act.wait_ge(mask_checked, 2 if i < 6 else 3)
                if i >= 2:
                    act.wait_ge(parts_summed, i - 1)
                nc.scalar.activation(junk[:, i % 2 * (N // PARTS):(i % 2 + 1) * (N // PARTS)], part[i], ACT.Identity,
                                     accum_out=part_sums[:, i // PARTS, i % PARTS:i % PARTS + 1]).then_inc(parts_summed, 1)

            def read_product(into, c, banks, before):
                act.wait_ge(products, before + c + 1)
                nc.scalar.copy(into[:, c, :], banks[c][:, :]).then_inc(products_read, 1)

            act.wait_ge(consts_made, 1)
            act.wait_ge(weights_in, 16 * 5)
            wide = [out_t[0], out_t[1]]
            for i, b in enumerate((0, 2)):
                for c in range(C):
                    nc.scalar.activation(wide[i][:, c * P:(c + 1) * P], ones[:, :], ACT.Copy,
                                         scale=bias_cols[:, b, c:c + 1]).then_inc(wide_made, 1)
            make_h(0, 0, x_in[0], 16)
            read_product(w_scores, 0, p_scores_weights, 0)
            check_mask(0, 0)
            for c in range(1, C):
                read_product(w_scores, c, p_scores_weights, 0)
            act.wait_ge(products, C + 1)
            nc.scalar.copy(b_scores[:, :], p_ctx[:, :]).then_inc(products_read, 1)
            nc.scalar.activation(w_shift[:, :], p_shift[:, 0:C], ACT.Copy, scale=INV)
            nc.scalar.activation(b_shift[:, :], p_shift[:, C:C + 1], ACT.Copy, scale=INV).then_inc(products_read, 1)
            turn_h(0)
            make_h(1, 1, x_in[1], 16)
            check_mask(0, 1)
            sum_part(0)
            turn_h(1)
            def read_out(t, u, b):
                act.wait_ge(out_summed, t + 1)
                act.wait_ge(out_stored[b], 16 * u + 16)
                nc.scalar.copy(out_t[b][:, :], p_out[:, :]).then_inc(out_read, 1)

            for i in range(1, 4):
                sum_part(i)
            for c in range(2):
                read_product(w_out, c, p_out_weights, C + 1)
                sum_part(4 + c)
            exponentials(0, masked[0], e_t[0])
            for c in range(2, C):
                read_product(w_out, c, p_out_weights, C + 1)
            act.wait_ge(products, 2 * C + 2)
            nc.scalar.copy(b_out[:, :], p_out_weights[0][:, :]).then_inc(products_read, 1)
            diagonals(0, SLOTS)
            make_h(2, 0, x_in[0], 32)
            check_mask(1, 0)
            turn_h(2)
            for i in range(6, C * PARTS):
                sum_part(i)
            act.wait_ge(parts_summed, C * PARTS)
            for i in range(C * PARTS):
                last = nc.scalar.activation(spread[:, i, :], ident[:, :], ACT.Copy,
                                            scale=part_sums[:, i // PARTS, i % PARTS:i % PARTS + 1])
            last.then_inc(parts_spread, 1)
            exponentials(1, masked[0], e_t[0])
            act.wait_ge(products, PRODUCTS - 1)
            nc.scalar.copy(value_sum, p_spare[:, :]).then_inc(products_read, 1)
            check_mask(1, 1)
            read_ctx(0)
            make_h(3, 1, x_in[1], 32)
            turn_ctx(0)

            def step(u, b, ahead=True):
                t = 2 * u + b
                diagonals(t - 1, SLOTS)
                read_out(t - 2, u - 1, b)
                if ahead:
                    check_mask(u + 1, b)
                turn_h(t + 1)
                read_ctx(t - 1)
                if ahead:
                    make_h(t + 2, b, x_in[b], 16 * u + 32)
                turn_ctx(t - 1)
                exponentials(t, masked[0], e_t[0])

            with act.Fori(1, T // 2 - 1) as u:
                step(u, 0)
                step(u, 1)
            step(T // 2 - 1, 0, ahead=False)
            diagonals(LAST - 1, SLOTS)
            read_out(LAST - 2, T // 2 - 2, 1)
            read_ctx(LAST - 1)
            turn_ctx(LAST - 1)
            exponentials(LAST, masked[0], e_t[0])
            make_h(T, 0, rest_in, 16)
            turn_h(T)
            diagonals(LAST, SLOTS)
            read_out(LAST - 1, T // 2 - 1, 0)
            read_ctx(LAST)
            turn_ctx(LAST)
            read_out(LAST, T // 2 - 1, 1)
            exponentials(T, masked[1], e_t[1])
            diagonals(T, SLOTS)
            turn_ctx(T)
            dense_scalar(act)

        @block.vector
        def _(dve):
            def find_largest(b, g):
                nc.vector.max(cand[:, g, :], mask[b][:, g * GW:(g + 1) * GW]).then_inc(scan_step, 1)

            def find_columns(t, b):
                alone(dve, (scan_step, SCAN * t + GROUPS))
                for g in range(GROUPS):
                    ins = nc.vector.max_index(where[:, g, :], cand[:, g, :], mask[b][:, g * GW:(g + 1) * GW])
                    ins.then_inc(scan_step if g < GROUPS - 1 else mask_scanned, 1)

            FOUND = 2 * GROUPS - 1

            def make_keys(t):
                dve.wait_ge(mask_scanned, t + 1)
                nc.vector.tensor_tensor(key_of[:, :, :], group_top[:, :, :], where[:, :, :], ALU.subtract).then_inc(scan_step, 1)

            def keep_edges(t):
                dve.wait_ge(scan_step, SCAN * t + FOUND + 1)
                nc.vector.scalar_tensor_tensor(edge_key[:, :, :], cand[:, :, :], 0.0, key_of[:, :, :],
                                               ALU.is_gt, ALU.mult).then_inc(scan_step, 1)

            def first_top(t):
                alone(dve, (scan_step, SCAN * t + FOUND + 2))
                nc.vector.max(top_key[:, 0:TOP], edge_key[:, :, :]).then_inc(scan_step, 1)

            def drop_top(t):
                alone(dve, (scan_step, SCAN * t + FOUND + 3))
                nc.vector.match_replace(later_key[:, :, :], top_key[:, 0:TOP], edge_key[:, :, :], 0.0).then_inc(scan_step, 1)

            def second_top(t):
                alone(dve, (scan_step, SCAN * t + FOUND + 4))
                nc.vector.max(top_key[:, TOP:REST], later_key[:, :, :]).then_inc(scan_step, 1)

            def make_record(t, u, b):
                dve.wait_ge(scan_step, SCAN * t + FOUND + 5)
                if not (isinstance(u, int) and u == 0):
                    dve.wait_ge(recorded[b], 16 * u)
                nc.vector.tensor_scalar(record[b][:, 0:REST], top_key[:, :], -1.0, float(N), ALU.mult, ALU.add).then_inc(columns_made, 1)
                nc.vector.tensor_scalar(used[b][:, :], top_key[:, :], 0.0, None, ALU.is_gt).then_inc(used_made, 1)

            def record_row(t, b):
                nc.vector.tensor_copy(record[b][:, REST:REST + 1], row_numbers[:, bass.ds(t, 1)]).then_inc(scan_step, 1)

            def find_more(t):
                nc.vector.scalar_tensor_tensor(more_all[:, bass.ds(t, 1), :].rearrange("p a n -> p (a n)"),
                                               edge_key[:, :, :].rearrange("p g n -> p (g n)"), top_key[:, REST - 1:REST],
                                               edge_key[:, :, :].rearrange("p g n -> p (g n)"),
                                               ALU.is_lt, ALU.mult).then_inc(scan_step, 1)

            def find_expected():
                nc.vector.tensor_tensor(is_expected[:, :, :], cand[:, :, :], expected[:, :, :], ALU.is_equal).then_inc(scan_step, 1)

            def find_odd(t):
                dve.wait_ge(scan_step, SCAN * t + FOUND + 8)
                nc.vector.tensor_tensor(odd_all[:, bass.ds(t, 1), :].rearrange("p a n -> p (a n)"),
                                        is_expected[:, :, :].rearrange("p g n -> p (g n)"),
                                        cand[:, :, :].rearrange("p g n -> p (g n)"), ALU.not_equal).then_inc(scan_step, 1)

            def make_place(t, b):
                dve.wait_ge(place_summed, t + 1)
                nc.vector.tensor_scalar(place_of[b][:, :], p_place[:, 0:1], float(FAR), None, ALU.add).then_inc(place_made, 1)

            def count_flagged(b):
                nc.vector.tensor_tensor(flagged[:, :], flagged[:, :], used[b][:, SLOTS:SLOTS + 1], ALU.add).then_inc(flagged_made, 1)

            def read_q(t):
                dve.wait_ge(q_summed, t + 1)
                dve.wait_ge(rstd_made, t + 1)
                nc.vector.scalar_tensor_tensor(q_t[:, :], p_proj[:, :], rstd[:, :], b_scores[:, :],
                                               ALU.mult, ALU.add).then_inc(q_made, 1)

            def read_shift(t):
                dve.wait_ge(shift_summed, t + 1)
                nc.vector.scalar_tensor_tensor(shift[:, :], p_shift[:, 0:1], rstd[:, :], b_shift[:, :],
                                               ALU.mult, ALU.add).then_inc(q_made, 1)

            def dot(t, i, s, key_rows):
                if i == 0:
                    dve.wait_ge(q_made, 2 * t + 2)
                if i >= 2:
                    dve.wait_ge(dot_step, DOTS * t + i - 1)
                nc.vector.tensor_tensor_reduce(out=product[i % 2], in0=key_rows, in1=q_t[:, :],
                                               scale=INV, scalar=0.0, op0=ALU.mult, op1=ALU.add,
                                               accum_out=dots[:, s:s + 1]).then_inc(dot_step, 1)

            def add_shift(t, used_t, slots):
                dve.wait_ge(dot_step, DOTS * t + slots)
                nc.vector.scalar_tensor_tensor(scaled[:, 0:slots], dots[:, 0:slots], shift[:, :], used_t[:, 0:slots],
                                               ALU.add, ALU.mult).then_inc(dot_step, 1)

            def below_threshold(t, slots):
                dve.wait_ge(dot_step, DOTS * t + slots + 1)
                nc.vector.tensor_scalar(low[:, 0:slots], scaled[:, 0:slots], THRESHOLD, MASKED, ALU.is_lt, ALU.mult).then_inc(dot_step, 1)

            def above_minus_threshold(t, slots):
                dve.wait_ge(dot_step, DOTS * t + slots + 2)
                nc.vector.scalar_tensor_tensor(low[:, 0:slots], scaled[:, 0:slots], -THRESHOLD, low[:, 0:slots],
                                               ALU.is_gt, ALU.mult).then_inc(dot_step, 1)

            def mask_low(t, masked_t, slots):
                dve.wait_ge(dot_step, DOTS * t + slots + 3)
                nc.vector.tensor_tensor(masked_t[:, 0:slots], scaled[:, 0:slots], low[:, 0:slots], ALU.add).then_inc(dot_step, 1)

            def maximum(t, masked_t, slots):
                dve.wait_ge(dot_step, DOTS * t + slots + 4)
                nc.vector.reduce_max(row_max[:, :], masked_t[:, :], AX.X).then_inc(dot_step, 1)

            def maximum_out(t, slots):
                dve.wait_ge(dot_step, DOTS * t + slots + 5)
                nc.vector.tensor_scalar(neg_max[:, :], row_max[:, :], -1.0, None, ALU.mult).then_inc(max_made, 1)

            def subtract_w0(t, e, slots):
                dve.wait_ge(exp_made, t + 1)
                nc.vector.tensor_scalar(above_w0[:, 0:slots], e[:, 0:slots], e[:, slots:slots + 1], 0.0,
                                        ALU.subtract, ALU.add, accum_out=weight_sum[:, :]).then_inc(dot_step, 1)

            def sum_row(t, e, slots):
                dve.wait_ge(dot_step, DOTS * t + slots + 6)
                nc.vector.scalar_tensor_tensor(row_sum[:, :], e[:, slots:slots + 1], float(N), weight_sum[:, :],
                                               ALU.mult, ALU.add).then_inc(dot_step, 1)

            def invert_sum(t, slots):
                dve.wait_ge(dot_step, DOTS * t + slots + 7)
                nc.vector.reciprocal(inv_sum[:, :], row_sum[:, :]).then_inc(dot_step, 1)

            def make_weights(t, e, slots):
                dve.wait_ge(dot_step, DOTS * t + slots + 8)
                nc.vector.tensor_tensor(w0[:, :], e[:, slots:slots + 1], inv_sum[:, :], ALU.mult).then_inc(dot_step, 1)
                nc.vector.tensor_scalar(weight[:, 0:slots], above_w0[:, 0:slots], inv_sum[:, :], None, ALU.mult).then_inc(weights_made, 1)

            def weights(t, e, slots):
                subtract_w0(t, e, slots)
                sum_row(t, e, slots)
                invert_sum(t, slots)
                make_weights(t, e, slots)

            def end_scores(t, used_t, masked_t, slots):
                add_shift(t, used_t, slots)
                below_threshold(t, slots)
                above_minus_threshold(t, slots)
                mask_low(t, masked_t, slots)
                maximum(t, masked_t, slots)
                maximum_out(t, slots)

            dve.wait_ge(consts_made, 1)
            alone(dve, (mask_in[0], 16))
            for g in range(GROUPS):
                find_largest(0, g)
            find_columns(0, 0)
            make_keys(0)
            keep_edges(0)
            first_top(0)
            drop_top(0)
            second_top(0)
            make_record(0, 0, 0)
            record_row(0, 0)
            find_more(0)
            find_expected()
            find_odd(0)

            alone(dve, (mask_in[1], 16), (scan_step, SCAN))
            for g in range(GROUPS):
                find_largest(1, g)
            find_columns(1, 1)
            make_keys(1)
            keep_edges(1)
            first_top(1)
            drop_top(1)
            second_top(1)
            make_record(1, 0, 1)
            record_row(1, 1)
            find_more(1)
            find_expected()
            find_odd(1)
            dve.wait_ge(products_read, C + 2)
            read_q(0)
            read_shift(0)
            make_place(0, 0)
            count_flagged(0)
            for s in range(SLOTS):
                if s % HALF == 0:
                    dve.wait_ge(edges_in[0][s // HALF], 16 * HALF)
                dot(0, s, s, edges[0][:, s, 0:D])
            end_scores(0, used[0], masked[0], SLOTS)

            def step(u, b):
                t = 2 * u + b
                un, bn = (u + 1, 0) if b else (u, 1)
                key_rows = [edges[b][:, s, 0:D] for s in range(SLOTS)]
                alone(dve, (mask_in[bn], 16 * un + 16), (scan_step, SCAN * (t + 1)))
                find_largest(bn, 0)
                subtract_w0(t - 1, e_t[0], SLOTS)
                make_place(t, b)
                sum_row(t - 1, e_t[0], SLOTS)
                count_flagged(b)
                invert_sum(t - 1, SLOTS)
                make_weights(t - 1, e_t[0], SLOTS)
                for g in range(1, GROUPS):
                    find_largest(bn, g)
                find_columns(t + 1, bn)
                read_q(t)
                make_keys(t + 1)
                read_shift(t)
                keep_edges(t + 1)
                dve.wait_ge(edges_in[b][0], 16 * HALF * u + 16 * HALF)
                dot(t, 0, 0, key_rows[0])
                first_top(t + 1)
                dot(t, 1, 1, key_rows[1])
                drop_top(t + 1)
                dot(t, 2, 2, key_rows[2])
                second_top(t + 1)
                dot(t, 3, 3, key_rows[3])
                make_record(t + 1, un, bn)
                dve.wait_ge(edges_in[b][1], 16 * HALF * u + 16 * HALF)
                for s in range(HALF, SLOTS):
                    dot(t, s, s, key_rows[s])
                record_row(t + 1, bn)
                add_shift(t, used[b], SLOTS)
                find_more(t + 1)
                below_threshold(t, SLOTS)
                find_expected()
                above_minus_threshold(t, SLOTS)
                find_odd(t + 1)
                mask_low(t, masked[0], SLOTS)
                maximum(t, masked[0], SLOTS)
                maximum_out(t, SLOTS)

            step(0, 1)
            with dve.Fori(1, T // 2 - 1) as u:
                step(u, 0)
                step(u, 1)
            step(T // 2 - 1, 0)

            make_place(LAST, 1)
            count_flagged(1)
            weights(LAST - 1, e_t[0], SLOTS)
            read_q(LAST)
            read_shift(LAST)
            for s in range(SLOTS):
                if s % HALF == 0:
                    dve.wait_ge(edges_in[1][s // HALF], 16 * HALF * (T // 2))
                dot(LAST, s, s, edges[1][:, s, 0:D])
            end_scores(LAST, used[1], masked[0], SLOTS)
            dve.wait_ge(rest_listed, 16)
            nc.vector.tensor_scalar(used[0][:, :], record[0][:, 0:REST], float(N), None, ALU.is_lt).then_inc(rest_used, 1)
            weights(LAST, e_t[0], SLOTS)
            read_q(T)
            read_shift(T)
            for i in range(REST):
                s = (SLOTS + i) % REST
                if i % HALF == 0:
                    dve.wait_ge(rest_edges_in[s // HALF], 16 * HALF)
                dot(T, i, s, rest_edges[s // SLOTS][:, s % SLOTS, 0:D])
            dve.wait_ge(rest_used, 1)
            end_scores(T, used[0], masked[1], REST)
            weights(T, e_t[1], REST)
            weighed = product[0]
            dve.wait_ge(weights_made, T + 1)
            for s in range(SLOTS, REST):
                rows = rest_edges[1][:, s - SLOTS, D:2 * D]
                if s == SLOTS:
                    nc.vector.tensor_scalar(weighed, rows, weight[:, s:s + 1], None, ALU.mult).then_inc(rest_step, 1)
                else:
                    dve.wait_ge(rest_step, s - SLOTS)
                    nc.vector.scalar_tensor_tensor(weighed, rows, weight[:, s:s + 1], weighed,
                                                   ALU.mult, ALU.add).then_inc(rest_step, 1)
            nc.vector.reduce_sum(verdict[:, 0:1], odd_all, AX.XY).then_inc(verdict_step, 1)
            nc.vector.reduce_sum(verdict[:, 1:2], more_all, AX.XY).then_inc(verdict_step, 1)
            dve.wait_ge(mask_checked, T)
            nc.vector.reduce_sum(verdict[:, 2:3], negatives[:, :], AX.X).then_inc(verdict_step, 1)
            dve.wait_ge(verdict_step, 3)
            nc.vector.reduce_sum(verdict[:, 3:4], verdict[:, 0:3], AX.X).then_inc(verdict_step, 1)
            dve.wait_ge(verdict_step, 4)
            nc.vector.tensor_scalar(verdict[:, 4:5], verdict[:, 3:4], 0.0, None, ALU.is_equal).then_inc(verdict_step, 1)
            dve.wait_ge(rest_step, REST - SLOTS)
            dve.wait_ge(ctx_summed, T + 1)
            nc.vector.tensor_tensor(ctx_t[:, :], p_ctx[:, :], weighed, ALU.add).then_inc(ctx_made, 1)
            dve.wait_ge(out_summed, T + 1)
            dve.wait_ge(x_bias_made, T + 1)
            dve.wait_ge(out_stored[0], 16 * (T // 2) + 16)
            nc.vector.tensor_tensor(out_t[0][:, :], p_out[:, :], x_bias[0][:, :], ALU.add).then_inc(rest_made, 1)
            dve.wait_ge(verdict_summed, 1)
            nc.vector.tensor_scalar(verdict[:, 5:6], p_place[:, 1:2], float(P), None, ALU.is_equal).then_inc(verdict_step, 1)
            nc.vector.tensor_scalar(verdict[:, 6:7], p_place[:, 2:3], float(P), None, ALU.is_le).then_inc(verdict_step, 1)
            dve.wait_ge(verdict_step, 7)
            nc.vector.tensor_tensor(verdict_i[:, :], verdict[:, 5:6], verdict[:, 6:7], ALU.mult).then_inc(verdict_made, 1)
            dense_vector(dve)

        @block.tensor
        def _(pe):
            def turn_h(t):
                pe.wait_ge(h_made, t + 1)
                for c in range(C):
                    last = nc.tensor.transpose(p_turn[:, c * P:(c + 1) * P], h_t[:, c * P:(c + 1) * P], ident[:, :])
                last.then_inc(h_turned, 1)

            def multiply_h(t):
                pe.wait_ge(hT_made, t + 1)
                if not (isinstance(t, int) and t == 0):
                    pe.wait_ge(q_made, 2 * t)
                for c in range(C):
                    last = nc.tensor.matmul(p_proj[:, :], hT[:, c, :], w_scores[:, c, :], start=(c == 0), stop=(c == C - 1))
                last.then_inc(q_summed, 1)

            def sum_shift():
                for c in range(C):
                    last = nc.tensor.matmul(p_shift[:, 0:1], hT[:, c, :], w_shift[:, c:c + 1],
                                            start=(c == 0), stop=(c == C - 1))
                last.then_inc(shift_summed, 1)

            def project_q(t):
                turn_h(t)
                multiply_h(t)
                sum_shift()

            def place(t, b, first=False):
                pe.wait_ge(used_made, t + 1)
                if not first:
                    pe.wait_ge(flagged_made, t)
                nc.tensor.matmul(p_place[:, 0:1], before[:, :], used[b][:, SLOTS:SLOTS + 1], start=True, stop=False)
                nc.tensor.matmul(p_place[:, 0:1], ones[:, :], flagged[:, :], start=False, stop=True).then_inc(place_summed, 1)

            def turn_ctx(t):
                pe.wait_ge(ctx_made, t + 1)
                for c in range(C):
                    last = nc.tensor.transpose(p_turn_ctx[:, c * P:(c + 1) * P], ctx_t[:, c * P:(c + 1) * P], ident[:, :])
                last.then_inc(ctx_turned, 1)

            def multiply_ctx(t):
                pe.wait_ge(ctxT_made, t + 1)
                if not (isinstance(t, int) and t == 0):
                    pe.wait_ge(out_read, t)
                for c in range(C):
                    last = nc.tensor.matmul(p_out[:, :], ctxT[:, c, :], w_out[:, c, :], start=(c == 0), stop=(c == C - 1))
                last.then_inc(out_summed, 1)

            def project_out(t):
                turn_ctx(t)
                multiply_ctx(t)

            def weigh(t, value_rows, others=True):
                for s, rows in enumerate(value_rows):
                    if s % HALF == 0:
                        pe.wait_ge(diag_made, 2 * t + s // HALF + 1)
                    last = nc.tensor.matmul(p_ctx[:, :], diag[:, s, :], rows, start=(s == 0), stop=False)
                last.then_inc(edges_used, 1)
                if others:
                    weigh_others(t)

            def weigh_others(t):
                pe.wait_ge(diag_w0_made, t + 1)
                nc.tensor.matmul(p_ctx[:, :], diag_w0[:, :], value_sum, start=False, stop=True).then_inc(ctx_summed, 1)

            value_rows = [[edges[b][:, s, D:2 * D] for s in range(SLOTS)] for b in range(2)]

            def product_of(left, right, into):
                for c in range(C):
                    for k in range(C):
                        last = nc.tensor.matmul(into[c][:, :], raw[left][:, k, c * P:(c + 1) * P],
                                                raw[right][:, k, :], start=(k == 0), stop=(k == C - 1))
                    last.then_inc(products, 1)

            pe.wait_ge(weights_in, 16 * 5)
            product_of("wq", "wk", p_scores_weights)
            pe.wait_ge(wide_made, 2 * C)
            wide = [out_t[0], out_t[1]]
            for k in range(C):
                nc.tensor.matmul(p_ctx[:, :], wide[0][:, k * P:(k + 1) * P], raw["wk"][:, k, :],
                                 start=(k == 0), stop=(k == C - 1))
            for c in range(C):
                for k in range(C):
                    nc.tensor.matmul(p_shift[:, c:c + 1], raw["wq"][:, k, c * P:(c + 1) * P],
                                     bias_cols[:, 1, k:k + 1], start=(k == 0), stop=(k == C - 1))
            for k in range(C):
                last = nc.tensor.matmul(p_shift[:, C:C + 1], wide[0][:, k * P:(k + 1) * P], bias_cols[:, 1, k:k + 1],
                                        start=(k == 0), stop=(k == C - 1))
            last.then_inc(products, 1)
            pe.wait_ge(products_read, C + 2)
            project_q(0)
            place(0, 0, first=True)
            project_q(1)
            place(1, 1)
            pe.wait_ge(late_weights_in, 48)
            product_of("wv", "wmT", p_out_weights)
            pe.wait_ge(products_read, C + 3)
            for k in range(C):
                last = nc.tensor.matmul(p_out_weights[0][:, :], wide[1][:, k * P:(k + 1) * P], raw["wmT"][:, k, :],
                                        start=(k == 0), stop=(k == C - 1))
            last.then_inc(products, 1)
            pe.wait_ge(products_read, 2 * C + 2)
            weigh(0, value_rows[0], others=False)
            project_q(2)
            pe.wait_ge(parts_spread, 1)
            pe.wait_ge(products_read, 2 * C + 3)
            for c in range(C):
                for k in range(PARTS):
                    last = nc.tensor.matmul(p_spare[:, c * P:(c + 1) * P], ones[:, :], spread[:, c * PARTS + k, :],
                                            start=(k == 0), stop=(k == PARTS - 1))
            last.then_inc(products, 1)
            place(2, 0)
            pe.wait_ge(products_read, PRODUCTS)
            weigh_others(0)
            project_out(0)

            def step(t, b):
                weigh(t - 1, value_rows[1 - b], others=False)
                turn_h(t + 1)
                weigh_others(t - 1)
                multiply_h(t + 1)
                turn_ctx(t - 1)
                sum_shift()
                place(t + 1, 1 - b)
                multiply_ctx(t - 1)

            with pe.Fori(2, LAST - 1, 2) as t:
                step(t, 0)
                step(t + 1, 1)
            step(LAST - 1, 0)
            weigh(LAST - 1, value_rows[0])
            project_out(LAST - 1)
            project_q(T)
            weigh(LAST, value_rows[1])
            project_out(LAST)
            weigh(T, value_rows[0])
            pe.wait_ge(verdict_step, 5)
            nc.tensor.matmul(p_place[:, 1:2], ones[:, :], verdict[:, 4:5], start=True, stop=True)
            nc.tensor.matmul(p_place[:, 2:3], ones[:, :], flagged[:, :], start=True, stop=True).then_inc(verdict_summed, 1)
            project_out(T)
            dense_tensor(pe)


def kernel(**inputs):
    import numpy as np
    import concourse.bacc as bacc
    from concourse.bass_utils import run_bass_kernel_spmd

    def down(b):
        return np.ascontiguousarray(b.reshape(-1, P).T)

    g = {n.removeprefix("L0_gnn_"): np.asarray(a) for n, a in inputs.items()}
    laid = {
        "x": g["x"], "adj": g["adj"], "keyT": g["key"].T, "valueT": g["value"].T,
        "kv": np.concatenate([g["key"], g["value"]], axis=1),
        "wq": g["Wq"], "wk": g["Wk"], "wv": g["Wv"], "wmT": g["Wm"].T,
        "bq": down(g["bq"]), "bk": down(g["bk"]), "bv": down(g["bv"]), "bm": g["bm"],
    }
    nc = bacc.Bacc("TRN2", target_bir_lowering=False, num_devices=1)
    arrays, args = {}, {}
    for name, a in laid.items():
        a = np.ascontiguousarray(a)
        arrays[f"in_{name}"] = a
        args[name] = nc.dram_tensor(f"in_{name}", a.shape, mybir.dt.from_np(a.dtype), kind="ExternalInput").ap()
    args["records"] = nc.dram_tensor("records", (P, REST + 1), U32, kind="Internal").ap()
    args["out"] = nc.dram_tensor("out_0", g["x"].shape, F32, kind="ExternalOutput").ap()
    graph_attention(nc, **args)
    r = run_bass_kernel_spmd(nc, [arrays], core_ids=[0])
    return r.results[0]["out_0"]
```
